# Optimizing a Trainium2 kernel written in Bass

```python
import numpy as np
import jax
import jax.numpy as jnp

def _softmax(x, axis=-1):
    return jax.nn.softmax(x, axis=axis)

def _gelu(x):
    return jax.nn.gelu(x, approximate=True)

def _silu(x):
    return jax.nn.silu(x)

def _sigmoid(x):
    return jax.nn.sigmoid(x)

def _layernorm(x, axis=-1, eps=1e-05):
    m = jnp.mean(x, axis=axis, keepdims=True)
    v = jnp.var(x, axis=axis, keepdims=True)
    return (x - m) / jnp.sqrt(v + eps)

def _scatter_add(tgt, idx, src, axis=0):
    return tgt.at[idx].add(src)

def _segment_sum(src, seg, n):
    return jax.ops.segment_sum(src, seg, n)
kernel_name = 'mk_xattn_ffn_d4_seqx_r8_44770b'

def setup_inputs(seed: int=0):
    np.random.seed(seed)
    _w = jnp.asarray

    def _rec_inputs():
        import jax
        import jax.numpy as jnp
        _rk = jax.random.key(seed)
        x = 7.22e-05 + 1 * jax.random.normal(jax.random.fold_in(_rk, 1), (128, 64, 128), jnp.float32)
        _lenS = 64 - jax.random.randint(jax.random.fold_in(_rk, 7), (128,), 0, max(1, 64 // 4) + 1, jnp.int32)
        _lenS2 = 64 - jax.random.randint(jax.random.fold_in(_rk, 8), (128,), 0, max(1, 64 // 4) + 1, jnp.int32)
        _ctx_1024P = jax.random.normal(jax.random.fold_in(_rk, 11), (128, 16, 128), jnp.float32)
        _ctx_1024c = jax.random.dirichlet(jax.random.fold_in(_rk, 511), 0.3 * jnp.ones((16,), jnp.float32), (128, 64))
        _ctx_1024t = jnp.einsum('bsk,bkd->bsd', _ctx_1024c, _ctx_1024P)
        _ctx_1024t = _ctx_1024t * jax.lax.rsqrt(jnp.mean(jnp.square(_ctx_1024t)) + 1e-12) * 0.953939
        ctx_1024 = 4.13588e-05 + 0.999923 * (_ctx_1024t + 0.3 * jax.random.normal(jax.random.fold_in(_rk, 611), (128, 64, 128), jnp.float32))
        itok_BxS_0_4095 = jax.random.randint(jax.random.fold_in(_rk, 12), (128, 64), 0, 512, jnp.int32)
        itok_BxS_0_511 = jax.random.randint(jax.random.fold_in(_rk, 13), (128, 64), 0, 64, jnp.int32)
        return (x, ctx_1024, itok_BxS_0_4095, itok_BxS_0_511)
    x, ctx_1024, itok_BxS_0_4095, itok_BxS_0_511 = _rec_inputs()

    def _L0_xattn_setup():
        import jax, jax.numpy as jnp
        import numpy as np
        B, L, DM, H = (2, 512, 128, 16)
        D = DM // H

        def _split_heads(x):
            b, l, _ = x.shape
            return x.reshape(b, l, H, D).transpose(0, 2, 1, 3)
        key = jax.random.key(seed)
        ks = jax.random.split(key, 11)
        s = 1.0 / np.sqrt(DM)
        return {'query': jax.random.normal(ks[0], (B, L, DM), jnp.float32), 'key': jax.random.normal(ks[1], (B, L, DM), jnp.float32), 'value': jax.random.normal(ks[2], (B, L, DM), jnp.float32), 'Wq': jax.random.normal(ks[3], (DM, DM), jnp.float32) * s, 'bq': jnp.zeros((DM,), jnp.float32), 'Wk': jax.random.normal(ks[4], (DM, DM), jnp.float32) * s, 'bk': jnp.zeros((DM,), jnp.float32), 'Wv': jax.random.normal(ks[5], (DM, DM), jnp.float32) * s, 'bv': jnp.zeros((DM,), jnp.float32), 'Wo': jax.random.normal(ks[6], (DM, DM), jnp.float32) * s, 'bo': jnp.zeros((DM,), jnp.float32)}
    _L0_xattn_all = _L0_xattn_setup()
    _L0_xattn_in = {k: v for k, v in _L0_xattn_all.items() if k in ('Wq', 'bq', 'Wk', 'bk', 'Wv', 'bv', 'Wo', 'bo')}
    del _L0_xattn_all

    def _L0_ffn_setup():
        import jax, jax.numpy as jnp
        import numpy as np
        EPS = 1e-05

        def rmsnorm(x):
            return x * jax.lax.rsqrt(jnp.mean(x * x, axis=-1, keepdims=True) + EPS)

        def act_quant(x):
            scale = 127.0 / jnp.clip(jnp.max(jnp.abs(x), axis=-1, keepdims=True), 1e-05)
            q = jnp.clip(jnp.round(x * scale), -128.0, 127.0) / scale
            return x + jax.lax.stop_gradient(q - x)

        def weight_quant(w):
            scale = 1.0 / jnp.clip(jnp.mean(jnp.abs(w)), 1e-05)
            q = jnp.clip(jnp.round(w * scale), -1.0, 1.0) / scale
            return w + jax.lax.stop_gradient(q - w)

        def bitlinear(x, w, b):
            xq = act_quant(rmsnorm(x))
            wq = weight_quant(w)
            return jnp.einsum('bsd,fd->bsf', xq, wq) + b
        key = jax.random.key(seed)
        k0, k1, k2 = jax.random.split(key, 3)
        B, S, D, F = (2, 1024, 128, 512)
        x = jax.random.normal(k0, (B, S, D), dtype=jnp.float32)
        w1 = jax.random.normal(k1, (F, D), dtype=jnp.float32) * (1.0 / np.sqrt(D))
        b1 = jnp.zeros((F,), dtype=jnp.float32)
        w2 = jax.random.normal(k2, (D, F), dtype=jnp.float32) * (1.0 / np.sqrt(F))
        b2 = jnp.zeros((D,), dtype=jnp.float32)
        return {'x': x, 'w1': w1, 'b1': b1, 'w2': w2, 'b2': b2}
    _L0_ffn_all = _L0_ffn_setup()
    _L0_ffn_in = {k: v for k, v in _L0_ffn_all.items() if k in ('w1', 'b1', 'w2', 'b2')}
    del _L0_ffn_all

    def _L1_xattn_setup():
        import jax, jax.numpy as jnp
        import numpy as np
        MODEL_DIM = 128
        NUM_HEADS = 16
        HEAD_DIM = MODEL_DIM // NUM_HEADS
        B, T = (4, 256)
        key = jax.random.key(seed)
        ks = jax.random.split(key, 11)
        s = 1.0 / np.sqrt(MODEL_DIM)

        def lin(kw, kb):
            W = jax.random.uniform(kw, (MODEL_DIM, MODEL_DIM), jnp.float32, -s, s)
            b = jax.random.uniform(kb, (MODEL_DIM,), jnp.float32, -s, s)
            return (W, b)
        Wq, bq = lin(ks[0], ks[1])
        Wk, bk = lin(ks[2], ks[3])
        Wv, bv = lin(ks[4], ks[5])
        Wo, bo = lin(ks[6], ks[7])
        query = jax.random.normal(ks[8], (B, T, MODEL_DIM), jnp.float32)
        key_t = jax.random.normal(ks[9], (B, T, MODEL_DIM), jnp.float32)
        value = jax.random.normal(ks[10], (B, T, MODEL_DIM), jnp.float32)
        return {'query': query, 'key': key_t, 'value': value, 'Wq': Wq, 'bq': bq, 'Wk': Wk, 'bk': bk, 'Wv': Wv, 'bv': bv, 'Wo': Wo, 'bo': bo}
    _L1_xattn_all = _L1_xattn_setup()
    _L1_xattn_in = {k: v for k, v in _L1_xattn_all.items() if k in ('Wq', 'bq', 'Wk', 'bk', 'Wv', 'bv', 'Wo', 'bo')}
    del _L1_xattn_all

    def _L1_ffn_setup():
        import jax, jax.numpy as jnp
        import numpy as np
        import math
        HID, HD, E, MIN_E = (128, 128, 16, 2)
        B, T = (4, 256)
        IS_CAUSAL = True

        def _l2norm(x, axis):
            return x / jnp.sqrt(jnp.sum(x * x, axis=axis, keepdims=True) + 1e-12)

        def _gating(hidden_states, sim_matrix, gates):
            b, t, c = hidden_states.shape
            flat = hidden_states.reshape(b * t, c)
            logits = _l2norm(flat, -1) @ _l2norm(sim_matrix, 0) - jax.nn.sigmoid(gates)
            gated = jax.nn.relu(logits)
            mask = (gated > 0).astype(gated.dtype)
            inactive = jnp.sum(mask, axis=1) == 0
            _, top_idx = jax.lax.top_k(logits, MIN_E)
            fb = jnp.sum(jax.nn.one_hot(top_idx, E, dtype=mask.dtype), axis=1)
            mask = mask + inactive[:, None].astype(mask.dtype) * fb
            masked = jnp.where(mask > 0, gated, -jnp.inf)
            probs = jax.nn.softmax(masked, axis=-1)
            return probs
        key = jax.random.key(seed)
        ks = jax.random.split(key, 6)
        a_qkv = math.sqrt(6.0 / (HID + HD))
        a_o = math.sqrt(6.0 / (HD + HID))
        return {'hidden_states': jax.random.normal(ks[0], (B, T, HID), jnp.float32), 'sim_matrix': jax.random.normal(ks[1], (HID, E), jnp.float32), 'gates': jnp.zeros((E,), jnp.float32), 'q_proj': jax.random.uniform(ks[2], (E, HID, HD), jnp.float32, -a_qkv, a_qkv), 'k_proj': jax.random.uniform(ks[3], (E, HID, HD), jnp.float32, -a_qkv, a_qkv), 'v_proj': jax.random.uniform(ks[4], (E, HID, HD), jnp.float32, -a_qkv, a_qkv), 'o_proj': jax.random.uniform(ks[5], (E, HD, HID), jnp.float32, -a_o, a_o)}
    _L1_ffn_all = _L1_ffn_setup()
    _L1_ffn_in = {k: v for k, v in _L1_ffn_all.items() if k in ('sim_matrix', 'gates', 'q_proj', 'k_proj', 'v_proj', 'o_proj')}
    del _L1_ffn_all

    def _L2_xattn_setup():
        import jax, jax.numpy as jnp
        import numpy as np
        N_HEAD = 16
        key = jax.random.key(seed)
        ks = jax.random.split(key, 5)
        b, l, d = (4, 256, 128)
        dh = d // N_HEAD
        return {'q': jax.random.normal(ks[0], (b, l, d), dtype=jnp.float32), 'kv': jax.random.normal(ks[1], (b, l, d), dtype=jnp.float32), 'Wq': jax.random.normal(ks[2], (d, d), dtype=jnp.float32) * 0.02, 'Wkv': jax.random.normal(ks[3], (2 * dh, d), dtype=jnp.float32) * 0.02, 'Wc': jax.random.normal(ks[4], (d, d), dtype=jnp.float32) * 0.02}
    _L2_xattn_all = _L2_xattn_setup()
    _L2_xattn_in = {k: v for k, v in _L2_xattn_all.items() if k in ('Wq', 'Wkv', 'Wc')}
    del _L2_xattn_all

    def _L2_ffn_setup():
        import math
        import jax, jax.numpy as jnp
        import numpy as np
        HIDDEN = 128
        INTER = 512
        EXPERTS = 8
        B, T = (4, 256)
        EPS = 1e-12
        CAP_FACTOR = 1.0
        MIN_CAP = 4

        def layer_norm(x, g, b, eps=EPS):
            m = jnp.mean(x, axis=-1, keepdims=True)
            v = jnp.var(x, axis=-1, keepdims=True)
            return (x - m) * jax.lax.rsqrt(v + eps) * g + b

        def top1_gate(x, wg, capacity):
            logits = x @ wg
            gates = jax.nn.softmax(logits, axis=-1)
            E = wg.shape[-1]
            idx = jnp.argmax(gates, axis=-1)
            mask1 = jax.nn.one_hot(idx, E, dtype=gates.dtype)
            locations = jnp.cumsum(mask1, axis=0) - mask1
            mask1 = mask1 * (locations < capacity).astype(gates.dtype)
            gates1_s = jnp.sum(gates * mask1, axis=-1)
            loc_s = jnp.sum(locations * mask1, axis=-1).astype(jnp.int32)
            loc_oh = jax.nn.one_hot(loc_s, capacity, dtype=gates.dtype)
            combine = gates1_s[:, None, None] * mask1[:, :, None] * loc_oh[:, None, :]
            dispatch = jax.lax.stop_gradient((combine > 0).astype(x.dtype))
            return (combine, dispatch)
        key = jax.random.key(seed)
        ks = jax.random.split(key, 8)
        s = 0.02
        return {'x': jax.random.normal(ks[0], (B, T, HIDDEN), jnp.float32), 'attn_nw': jnp.ones((HIDDEN,), jnp.float32), 'attn_nb': jnp.zeros((HIDDEN,), jnp.float32), 'wg': jax.random.normal(ks[1], (HIDDEN, EXPERTS), jnp.float32) * s, 'inter_w': jax.random.normal(ks[2], (EXPERTS, HIDDEN, INTER), jnp.float32) * s, 'inter_b': jnp.zeros((EXPERTS, INTER), jnp.float32), 'output_w': jax.random.normal(ks[3], (EXPERTS, INTER, HIDDEN), jnp.float32) * s, 'output_b': jnp.zeros((EXPERTS, HIDDEN), jnp.float32), 'res_inter_w': jax.random.normal(ks[4], (HIDDEN, INTER), jnp.float32) * s, 'res_inter_b': jnp.zeros((INTER,), jnp.float32), 'res_output_w': jax.random.normal(ks[5], (INTER, HIDDEN), jnp.float32) * s, 'res_output_b': jnp.zeros((HIDDEN,), jnp.float32), 'res_coef': jax.random.normal(ks[6], (HIDDEN, 2), jnp.float32) * s}
    _L2_ffn_all = _L2_ffn_setup()
    _L2_ffn_in = {k: v for k, v in _L2_ffn_all.items() if k in ('attn_nw', 'attn_nb', 'wg', 'inter_w', 'inter_b', 'output_w', 'output_b', 'res_inter_w', 'res_inter_b', 'res_output_w', 'res_output_b', 'res_coef')}
    del _L2_ffn_all

    def _L3_xattn_setup():
        import jax, jax.numpy as jnp
        import numpy as np
        B, LQ, LK = (2, 512, 64)
        Q_DIM, KV_DIM, D_ATTN, N_HEADS = (128, 128, 128, 16)
        HDIM = D_ATTN // N_HEADS
        LOOKBACK = 4
        ROPE_MAX = 1024

        def rope_tables(smax, hdim):
            inv_freq = 1.0 / 10000.0 ** (jnp.arange(0, hdim, 2, dtype=jnp.float32) / hdim)
            freqs = jnp.arange(smax, dtype=jnp.float32)[:, None] * inv_freq[None, :]
            emb = jnp.concatenate([freqs, freqs], axis=-1)
            return (jnp.cos(emb), jnp.sin(emb))

        def rotate_half(x):
            h = x.shape[-1] // 2
            return jnp.concatenate([-x[..., h:], x[..., :h]], axis=-1)
        key = jax.random.key(seed)
        ks = jax.random.split(key, 8)
        q = jax.random.normal(ks[0], (B, LQ, Q_DIM), dtype=jnp.float32)
        kv = jax.random.normal(ks[1], (B, LK, KV_DIM), dtype=jnp.float32)
        q_pos_ids = jax.random.randint(ks[2], (B, LQ), 0, 512)
        kv_pos_ids = jax.random.randint(ks[3], (LK,), 0, 512)
        seg_id = jnp.sort(jax.random.randint(ks[4], (B, LQ), 0, LK), axis=-1)
        sc = 1.0 / np.sqrt(Q_DIM)
        Wq = jax.random.normal(ks[5], (Q_DIM, D_ATTN), dtype=jnp.float32) * sc
        Wkv = jax.random.normal(ks[6], (KV_DIM, 2 * D_ATTN), dtype=jnp.float32) * sc
        Wo = jax.random.normal(ks[7], (D_ATTN, Q_DIM), dtype=jnp.float32) * sc
        return {'q': q, 'kv': kv, 'q_pos_ids': q_pos_ids, 'kv_pos_ids': kv_pos_ids, 'seg_id': seg_id, 'Wq': Wq, 'Wkv': Wkv, 'Wo': Wo}
    _L3_xattn_all = _L3_xattn_setup()
    _L3_xattn_in = {k: v for k, v in _L3_xattn_all.items() if k in ('kv_pos_ids', 'Wq', 'Wkv', 'Wo')}
    del _L3_xattn_all

    def _L3_ffn_setup():
        import jax, jax.numpy as jnp
        import numpy as np

        def _ste(w, w_q):
            return w + jax.lax.stop_gradient(w_q - w)

        def quantize_w8_per(w, axis):
            amax = jnp.clip(jnp.max(jnp.abs(w), axis=axis, keepdims=True), 1e-08, None)
            scale = 127.0 / amax
            w_q = jnp.clip(jnp.round(w * scale), -128.0, 127.0) / scale
            return _ste(w, w_q)

        def quantize_a16(x):
            amax = jnp.clip(jnp.max(jnp.abs(x)), 1e-08, None)
            scale = 32767.0 / amax
            x_q = jnp.clip(jnp.round(x * scale), -32768.0, 32767.0) / scale
            return _ste(x, x_q)
        key = jax.random.key(seed)
        k1, k2, k3 = jax.random.split(key, 3)
        d_model, d_ff = (128, 512)
        x = jax.random.normal(k1, (4, 256, d_model), dtype=jnp.float32)
        W_in = jax.random.normal(k2, (d_model, d_ff), dtype=jnp.float32) / np.sqrt(d_model)
        b_in = jnp.zeros((d_ff,), dtype=jnp.float32)
        W_out = jax.random.normal(k3, (d_ff, d_model), dtype=jnp.float32) / np.sqrt(d_ff)
        b_out = jnp.zeros((d_model,), dtype=jnp.float32)
        return {'x': x, 'W_in': W_in, 'b_in': b_in, 'W_out': W_out, 'b_out': b_out}
    _L3_ffn_all = _L3_ffn_setup()
    _L3_ffn_in = {k: v for k, v in _L3_ffn_all.items() if k in ('W_in', 'b_in', 'W_out', 'b_out')}
    del _L3_ffn_all
    return {'x': x, 'ctx_1024': ctx_1024, 'itok_BxS_0_4095': itok_BxS_0_4095, 'itok_BxS_0_511': itok_BxS_0_511, 'L0_xattn_Wq': _L0_xattn_in['Wq'], 'L0_xattn_bq': _L0_xattn_in['bq'], 'L0_xattn_Wk': _L0_xattn_in['Wk'], 'L0_xattn_bk': _L0_xattn_in['bk'], 'L0_xattn_Wv': _L0_xattn_in['Wv'], 'L0_xattn_bv': _L0_xattn_in['bv'], 'L0_xattn_Wo': _L0_xattn_in['Wo'], 'L0_xattn_bo': _L0_xattn_in['bo'], 'L0_ffn_w1': _L0_ffn_in['w1'], 'L0_ffn_b1': _L0_ffn_in['b1'], 'L0_ffn_w2': _L0_ffn_in['w2'], 'L0_ffn_b2': _L0_ffn_in['b2'], 'L1_xattn_Wq': _L1_xattn_in['Wq'], 'L1_xattn_bq': _L1_xattn_in['bq'], 'L1_xattn_Wk': _L1_xattn_in['Wk'], 'L1_xattn_bk': _L1_xattn_in['bk'], 'L1_xattn_Wv': _L1_xattn_in['Wv'], 'L1_xattn_bv': _L1_xattn_in['bv'], 'L1_xattn_Wo': _L1_xattn_in['Wo'], 'L1_xattn_bo': _L1_xattn_in['bo'], 'L1_ffn_sim_matrix': _L1_ffn_in['sim_matrix'], 'L1_ffn_gates': _L1_ffn_in['gates'], 'L1_ffn_q_proj': _L1_ffn_in['q_proj'], 'L1_ffn_k_proj': _L1_ffn_in['k_proj'], 'L1_ffn_v_proj': _L1_ffn_in['v_proj'], 'L1_ffn_o_proj': _L1_ffn_in['o_proj'], 'L2_xattn_Wq': _L2_xattn_in['Wq'], 'L2_xattn_Wkv': _L2_xattn_in['Wkv'], 'L2_xattn_Wc': _L2_xattn_in['Wc'], 'L2_ffn_attn_nw': _L2_ffn_in['attn_nw'], 'L2_ffn_attn_nb': _L2_ffn_in['attn_nb'], 'L2_ffn_wg': _L2_ffn_in['wg'], 'L2_ffn_inter_w': _L2_ffn_in['inter_w'], 'L2_ffn_inter_b': _L2_ffn_in['inter_b'], 'L2_ffn_output_w': _L2_ffn_in['output_w'], 'L2_ffn_output_b': _L2_ffn_in['output_b'], 'L2_ffn_res_inter_w': _L2_ffn_in['res_inter_w'], 'L2_ffn_res_inter_b': _L2_ffn_in['res_inter_b'], 'L2_ffn_res_output_w': _L2_ffn_in['res_output_w'], 'L2_ffn_res_output_b': _L2_ffn_in['res_output_b'], 'L2_ffn_res_coef': _L2_ffn_in['res_coef'], 'L3_xattn_kv_pos_ids': _L3_xattn_in['kv_pos_ids'], 'L3_xattn_Wq': _L3_xattn_in['Wq'], 'L3_xattn_Wkv': _L3_xattn_in['Wkv'], 'L3_xattn_Wo': _L3_xattn_in['Wo'], 'L3_ffn_W_in': _L3_ffn_in['W_in'], 'L3_ffn_b_in': _L3_ffn_in['b_in'], 'L3_ffn_W_out': _L3_ffn_in['W_out'], 'L3_ffn_b_out': _L3_ffn_in['b_out']}

def reference(x, ctx_1024, itok_BxS_0_4095, itok_BxS_0_511, L0_xattn_Wq, L0_xattn_bq, L0_xattn_Wk, L0_xattn_bk, L0_xattn_Wv, L0_xattn_bv, L0_xattn_Wo, L0_xattn_bo, L0_ffn_w1, L0_ffn_b1, L0_ffn_w2, L0_ffn_b2, L1_xattn_Wq, L1_xattn_bq, L1_xattn_Wk, L1_xattn_bk, L1_xattn_Wv, L1_xattn_bv, L1_xattn_Wo, L1_xattn_bo, L1_ffn_sim_matrix, L1_ffn_gates, L1_ffn_q_proj, L1_ffn_k_proj, L1_ffn_v_proj, L1_ffn_o_proj, L2_xattn_Wq, L2_xattn_Wkv, L2_xattn_Wc, L2_ffn_attn_nw, L2_ffn_attn_nb, L2_ffn_wg, L2_ffn_inter_w, L2_ffn_inter_b, L2_ffn_output_w, L2_ffn_output_b, L2_ffn_res_inter_w, L2_ffn_res_inter_b, L2_ffn_res_output_w, L2_ffn_res_output_b, L2_ffn_res_coef, L3_xattn_kv_pos_ids, L3_xattn_Wq, L3_xattn_Wkv, L3_xattn_Wo, L3_ffn_W_in, L3_ffn_b_in, L3_ffn_W_out, L3_ffn_b_out):
    import jax
    import jax.numpy as jnp

    def _L0_xattn_ref(query, key, value, Wq, bq, Wk, bk, Wv, bv, Wo, bo):
        import jax, jax.numpy as jnp
        import numpy as np
        B, L, DM, H = (2, 512, 128, 16)
        D = DM // H

        def _split_heads(x):
            b, l, _ = x.shape
            return x.reshape(b, l, H, D).transpose(0, 2, 1, 3)
        q = _split_heads(query @ Wq + bq)
        k = _split_heads(key @ Wk + bk)
        v = _split_heads(value @ Wv + bv)
        q = jax.nn.elu(q) + 1.0
        k = jax.nn.elu(k) + 1.0
        S = jnp.einsum('bhle,bhld->bhed', k, q)
        out = jnp.einsum('bhme,bhed->bhmd', v, S)
        denom = jnp.einsum('bhld,bhld->bhl', q, k) + 1e-06
        out = out / denom[..., None]
        out = out.transpose(0, 2, 1, 3).reshape(out.shape[0], -1, DM)
        return out @ Wo + bo

    def _L0_ffn_ref(x, w1, b1, w2, b2):
        import jax, jax.numpy as jnp
        import numpy as np
        EPS = 1e-05

        def rmsnorm(x):
            return x * jax.lax.rsqrt(jnp.mean(x * x, axis=-1, keepdims=True) + EPS)

        def act_quant(x):
            scale = 127.0 / jnp.clip(jnp.max(jnp.abs(x), axis=-1, keepdims=True), 1e-05)
            q = jnp.clip(jnp.round(x * scale), -128.0, 127.0) / scale
            return x + jax.lax.stop_gradient(q - x)

        def weight_quant(w):
            scale = 1.0 / jnp.clip(jnp.mean(jnp.abs(w)), 1e-05)
            q = jnp.clip(jnp.round(w * scale), -1.0, 1.0) / scale
            return w + jax.lax.stop_gradient(q - w)

        def bitlinear(x, w, b):
            xq = act_quant(rmsnorm(x))
            wq = weight_quant(w)
            return jnp.einsum('bsd,fd->bsf', xq, wq) + b
        h = bitlinear(x, w1, b1)
        h = jax.nn.gelu(h, approximate=False)
        return bitlinear(h, w2, b2)

    def _L1_xattn_ref(query, key, value, Wq, bq, Wk, bk, Wv, bv, Wo, bo):
        import jax, jax.numpy as jnp
        import numpy as np
        MODEL_DIM = 128
        NUM_HEADS = 16
        HEAD_DIM = MODEL_DIM // NUM_HEADS
        B, T = (4, 256)
        b, tq, d = query.shape
        tk = key.shape[-2]
        h, hd = (NUM_HEADS, HEAD_DIM)
        q = (query @ Wq.T + bq).reshape(b, tq, h, hd)
        k = (key @ Wk.T + bk).reshape(b, tk, h, hd)
        v = (value @ Wv.T + bv).reshape(b, tk, h, hd)
        score = jnp.einsum('bqhd,bkhd->bhqk', q, k) / np.sqrt(hd).astype(np.float32)
        causal = jnp.tril(jnp.ones((tq, tk), dtype=bool))
        score = jnp.where(causal, score, -jnp.inf)
        probs = jax.nn.softmax(score, axis=-1)
        out = jnp.einsum('bhqk,bkhd->bqhd', probs, v).reshape(b, tq, d)
        return out @ Wo.T + bo

    def _L1_ffn_ref(hidden_states, sim_matrix, gates, q_proj, k_proj, v_proj, o_proj):
        import jax, jax.numpy as jnp
        import numpy as np
        import math
        HID, HD, E, MIN_E = (128, 128, 16, 2)
        B, T = (4, 256)
        IS_CAUSAL = True

        def _l2norm(x, axis):
            return x / jnp.sqrt(jnp.sum(x * x, axis=axis, keepdims=True) + 1e-12)

        def _gating(hidden_states, sim_matrix, gates):
            b, t, c = hidden_states.shape
            flat = hidden_states.reshape(b * t, c)
            logits = _l2norm(flat, -1) @ _l2norm(sim_matrix, 0) - jax.nn.sigmoid(gates)
            gated = jax.nn.relu(logits)
            mask = (gated > 0).astype(gated.dtype)
            inactive = jnp.sum(mask, axis=1) == 0
            _, top_idx = jax.lax.top_k(logits, MIN_E)
            fb = jnp.sum(jax.nn.one_hot(top_idx, E, dtype=mask.dtype), axis=1)
            mask = mask + inactive[:, None].astype(mask.dtype) * fb
            masked = jnp.where(mask > 0, gated, -jnp.inf)
            probs = jax.nn.softmax(masked, axis=-1)
            return probs
        b, t, c = hidden_states.shape
        rw = _gating(hidden_states, sim_matrix, gates).reshape(b, t, E)
        q = jnp.einsum('btc,ech,bte->bth', hidden_states, q_proj, rw)
        k = jnp.einsum('btc,ech,bte->bth', hidden_states, k_proj, rw)
        v = jnp.einsum('btc,ech,bte->bth', hidden_states, v_proj, rw)
        scale = 1.0 / math.sqrt(HD)
        scores = jnp.einsum('bqh,bkh->bqk', q, k) * scale
        if IS_CAUSAL:
            causal = jnp.tril(jnp.ones((t, t), dtype=bool))
            scores = jnp.where(causal[None], scores, -jnp.inf)
        attn = jax.nn.softmax(scores, axis=-1)
        ao = jnp.einsum('bqk,bkh->bqh', attn, v)
        out = jnp.einsum('bth,ehc,bte->btc', ao, o_proj, rw)
        return out

    def _L2_xattn_ref(q, kv, Wq, Wkv, Wc):
        import jax, jax.numpy as jnp
        import numpy as np
        N_HEAD = 16
        b, l, d = q.shape
        h = N_HEAD
        dh = d // h
        qp = jnp.einsum('bld,ed->ble', q, Wq)
        scores = jnp.einsum('bld,bmd->blm', qp, kv)
        idx = jnp.argmax(scores, axis=-1)
        mem = jnp.take_along_axis(kv, idx[..., None], axis=1)
        mkv = jnp.einsum('bld,ed->ble', mem, Wkv)
        mk, mv = jnp.split(mkv, 2, axis=-1)
        qh = qp.reshape(b, l, h, dh).transpose(0, 2, 1, 3)
        scale = 1.0 / np.sqrt(dh).astype(np.float32)
        logits = jnp.einsum('bhld,bmd->bhlm', qh, mk) * scale
        attn = jax.nn.softmax(logits, axis=-1)
        out = jnp.einsum('bhlm,bmd->bhld', attn, mv)
        out = out.transpose(0, 2, 1, 3).reshape(b, l, d)
        return jnp.einsum('bld,ed->ble', out, Wc)

    def _L2_ffn_ref(x, attn_nw, attn_nb, wg, inter_w, inter_b, output_w, output_b, res_inter_w, res_inter_b, res_output_w, res_output_b, res_coef):
        import math
        import jax, jax.numpy as jnp
        import numpy as np
        HIDDEN = 128
        INTER = 512
        EXPERTS = 8
        B, T = (4, 256)
        EPS = 1e-12
        CAP_FACTOR = 1.0
        MIN_CAP = 4

        def layer_norm(x, g, b, eps=EPS):
            m = jnp.mean(x, axis=-1, keepdims=True)
            v = jnp.var(x, axis=-1, keepdims=True)
            return (x - m) * jax.lax.rsqrt(v + eps) * g + b

        def top1_gate(x, wg, capacity):
            logits = x @ wg
            gates = jax.nn.softmax(logits, axis=-1)
            E = wg.shape[-1]
            idx = jnp.argmax(gates, axis=-1)
            mask1 = jax.nn.one_hot(idx, E, dtype=gates.dtype)
            locations = jnp.cumsum(mask1, axis=0) - mask1
            mask1 = mask1 * (locations < capacity).astype(gates.dtype)
            gates1_s = jnp.sum(gates * mask1, axis=-1)
            loc_s = jnp.sum(locations * mask1, axis=-1).astype(jnp.int32)
            loc_oh = jax.nn.one_hot(loc_s, capacity, dtype=gates.dtype)
            combine = gates1_s[:, None, None] * mask1[:, :, None] * loc_oh[:, None, :]
            dispatch = jax.lax.stop_gradient((combine > 0).astype(x.dtype))
            return (combine, dispatch)
        Bx, Tx, M = x.shape
        S = Bx * Tx
        E = wg.shape[-1]
        capacity = max(MIN_CAP, math.ceil(S / E * CAP_FACTOR))
        residual = x.reshape(S, M)
        attn_out = layer_norm(residual, attn_nw, attn_nb)
        combine, dispatch = top1_gate(attn_out, wg, capacity)
        dispatched = jnp.einsum('sec,sm->ecm', dispatch, attn_out)
        h = jax.nn.gelu(jnp.einsum('ecm,emi->eci', dispatched, inter_w) + inter_b[:, None, :], approximate=True)
        expert_out = jnp.einsum('eci,eim->ecm', h, output_w) + output_b[:, None, :]
        moe_out = jnp.einsum('sec,ecm->sm', combine, expert_out)
        rh = jax.nn.gelu(attn_out @ res_inter_w + res_inter_b, approximate=True)
        res_mlp_out = rh @ res_output_w + res_output_b
        coef = jax.nn.softmax(attn_out @ res_coef, axis=-1)
        out = res_mlp_out * coef[:, :1] + moe_out * coef[:, 1:]
        out = out + residual
        return out.reshape(Bx, Tx, M)

    def _L3_xattn_ref(q, kv, q_pos_ids, kv_pos_ids, seg_id, Wq, Wkv, Wo):
        import jax, jax.numpy as jnp
        import numpy as np
        B, LQ, LK = (2, 512, 64)
        Q_DIM, KV_DIM, D_ATTN, N_HEADS = (128, 128, 128, 16)
        HDIM = D_ATTN // N_HEADS
        LOOKBACK = 4
        ROPE_MAX = 1024

        def rope_tables(smax, hdim):
            inv_freq = 1.0 / 10000.0 ** (jnp.arange(0, hdim, 2, dtype=jnp.float32) / hdim)
            freqs = jnp.arange(smax, dtype=jnp.float32)[:, None] * inv_freq[None, :]
            emb = jnp.concatenate([freqs, freqs], axis=-1)
            return (jnp.cos(emb), jnp.sin(emb))

        def rotate_half(x):
            h = x.shape[-1] // 2
            return jnp.concatenate([-x[..., h:], x[..., :h]], axis=-1)
        Bq, Lq, _ = q.shape
        Lk = kv.shape[1]
        qh = (q @ Wq).reshape(Bq, Lq, N_HEADS, HDIM).transpose(0, 2, 1, 3)
        kvl = kv @ Wkv
        kh = kvl[..., :D_ATTN].reshape(Bq, Lk, N_HEADS, HDIM).transpose(0, 2, 1, 3)
        vh = kvl[..., D_ATTN:].reshape(Bq, Lk, N_HEADS, HDIM).transpose(0, 2, 1, 3)
        cos, sin = rope_tables(ROPE_MAX, HDIM)
        qp = jnp.clip(q_pos_ids, 0, ROPE_MAX - 1)
        q_cos = cos[qp][:, None]
        q_sin = sin[qp][:, None]
        qh = qh * q_cos + rotate_half(qh) * q_sin
        kp = jnp.clip(kv_pos_ids, 0, ROPE_MAX - 1)
        k_cos = cos[kp][None, None]
        k_sin = sin[kp][None, None]
        kh = kh * k_cos + rotate_half(kh) * k_sin
        kidx = jnp.arange(Lk)
        keep = (kidx[None, None, :] <= seg_id[:, :, None]) & (kidx[None, None, :] >= seg_id[:, :, None] - LOOKBACK)
        scale = 1.0 / np.sqrt(HDIM)
        scores = jnp.einsum('bhqd,bhkd->bhqk', qh, kh) * scale
        scores = jnp.where(keep[:, None], scores, -jnp.inf)
        attn = jax.nn.softmax(scores, axis=-1)
        ctx = jnp.einsum('bhqk,bhkd->bhqd', attn, vh)
        out = ctx.transpose(0, 2, 1, 3).reshape(Bq, Lq, D_ATTN)
        return out @ Wo

    def _L3_ffn_ref(x, W_in, b_in, W_out, b_out):
        import jax, jax.numpy as jnp
        import numpy as np

        def _ste(w, w_q):
            return w + jax.lax.stop_gradient(w_q - w)

        def quantize_w8_per(w, axis):
            amax = jnp.clip(jnp.max(jnp.abs(w), axis=axis, keepdims=True), 1e-08, None)
            scale = 127.0 / amax
            w_q = jnp.clip(jnp.round(w * scale), -128.0, 127.0) / scale
            return _ste(w, w_q)

        def quantize_a16(x):
            amax = jnp.clip(jnp.max(jnp.abs(x)), 1e-08, None)
            scale = 32767.0 / amax
            x_q = jnp.clip(jnp.round(x * scale), -32768.0, 32767.0) / scale
            return _ste(x, x_q)
        W_in_sim = quantize_w8_per(W_in, axis=0)
        W_out_sim = quantize_w8_per(W_out, axis=1)
        x_sim = quantize_a16(x)
        hidden = jax.nn.gelu(x_sim @ W_in_sim + b_in, approximate=False)
        hidden_sim = quantize_a16(hidden)
        out = hidden_sim @ W_out_sim + b_out
        return out
    x = x + _L0_xattn_ref(_layernorm(x, axis=-1), ctx_1024, ctx_1024, L0_xattn_Wq, L0_xattn_bq, L0_xattn_Wk, L0_xattn_bk, L0_xattn_Wv, L0_xattn_bv, L0_xattn_Wo, L0_xattn_bo)
    x = x + _L0_ffn_ref(_layernorm(x, axis=-1), L0_ffn_w1, L0_ffn_b1, L0_ffn_w2, L0_ffn_b2)
    x = x + _L1_xattn_ref(_layernorm(x, axis=-1), ctx_1024, ctx_1024, L1_xattn_Wq, L1_xattn_bq, L1_xattn_Wk, L1_xattn_bk, L1_xattn_Wv, L1_xattn_bv, L1_xattn_Wo, L1_xattn_bo)
    x = x + _L1_ffn_ref(_layernorm(x, axis=-1), L1_ffn_sim_matrix, L1_ffn_gates, L1_ffn_q_proj, L1_ffn_k_proj, L1_ffn_v_proj, L1_ffn_o_proj)
    x = x + _L2_xattn_ref(_layernorm(x, axis=-1), ctx_1024, L2_xattn_Wq, L2_xattn_Wkv, L2_xattn_Wc)
    x = x + _L2_ffn_ref(_layernorm(x, axis=-1), L2_ffn_attn_nw, L2_ffn_attn_nb, L2_ffn_wg, L2_ffn_inter_w, L2_ffn_inter_b, L2_ffn_output_w, L2_ffn_output_b, L2_ffn_res_inter_w, L2_ffn_res_inter_b, L2_ffn_res_output_w, L2_ffn_res_output_b, L2_ffn_res_coef)
    x = x + _L3_xattn_ref(_layernorm(x, axis=-1), ctx_1024, itok_BxS_0_4095, L3_xattn_kv_pos_ids, itok_BxS_0_511, L3_xattn_Wq, L3_xattn_Wkv, L3_xattn_Wo)
    x = x + _L3_ffn_ref(_layernorm(x, axis=-1), L3_ffn_W_in, L3_ffn_b_in, L3_ffn_W_out, L3_ffn_b_out)
    return x

_drawn_inputs = setup_inputs


def setup_inputs(seed=0):
    import zlib

    import numpy as np

    out = dict(_drawn_inputs(seed))
    spreads = {'L0_xattn_bq': (0.0, 0.1),
     'L0_xattn_bk': (0.0, 0.1),
     'L0_xattn_bv': (0.0, 0.1),
     'L0_xattn_bo': (0.0, 0.8),
     'L0_ffn_b1': (0.0, 0.8),
     'L0_ffn_b2': (0.0, 0.8),
     'L1_ffn_gates': (0.0, 0.8),
     'L2_ffn_attn_nw': (1.0, 0.6),
     'L2_ffn_attn_nb': (0.0, 0.8),
     'L2_ffn_inter_b': (0.0, 2.0),
     'L2_ffn_output_b': (0.0, 2.0),
     'L2_ffn_res_inter_b': (0.0, 2.0),
     'L2_ffn_res_output_b': (0.0, 2.0),
     'L3_ffn_b_in': (0.0, 0.8),
     'L3_ffn_b_out': (0.0, 2.0)}
    factors = {'L0_ffn_w1': 2.683,
     'L1_xattn_Wq': 8.0,
     'L1_xattn_bq': 8.0,
     'L1_xattn_Wk': 8.0,
     'L1_xattn_bk': 64.0,
     'L1_xattn_Wv': 8.0,
     'L1_xattn_bv': 8.0,
     'L1_xattn_Wo': 8.0,
     'L1_xattn_bo': 8.0,
     'L1_ffn_sim_matrix': 7.93,
     'L1_ffn_q_proj': 8.0,
     'L1_ffn_k_proj': 8.0,
     'L1_ffn_v_proj': 7.89,
     'L1_ffn_o_proj': 7.761,
     'L2_xattn_Wq': 8.0,
     'L2_xattn_Wkv': 8.0,
     'L2_xattn_Wc': 8.0,
     'L2_ffn_wg': 8.0,
     'L2_ffn_inter_w': 8.0,
     'L2_ffn_output_w': 8.0,
     'L2_ffn_res_inter_w': 8.0,
     'L2_ffn_res_output_w': 8.0,
     'L2_ffn_res_coef': 8.0,
     'L3_xattn_Wq': 25.031,
     'L3_ffn_W_in': 2.916,
     'L3_ffn_W_out': 2.735,
     'L3_xattn_Wkv': 3.111,
     'L3_xattn_Wo': 3.099}
    for name, (base, spread) in spreads.items():
        noise = np.random.default_rng([zlib.crc32(name.encode()), seed]).standard_normal(out[name].shape)
        drawn = base * np.exp(spread * noise) if base else spread * noise
        out[name] = jnp.asarray(drawn.astype(out[name].dtype))
    for name, factor in factors.items():
        out[name] = (out[name] * factor).astype(out[name].dtype)
    return out
```

```python
from contextlib import ExitStack
from collections import namedtuple

import concourse.bass as bass
import numpy as np
from concourse import mybir

ALU = mybir.AluOpType
ACT = mybir.ActivationFunctionType
AX_X = mybir.AxisListType.X
F32 = mybir.dt.float32
BF16 = mybir.dt.bfloat16
I32 = mybir.dt.int32

P = 128
D = 128
S = 64
H = 16
HD = D // H
TG = 4
GT = TG * P
SG = GT // S
LANES = 2
INV = 5
BANK = 512
F0 = 512
TILES_MAX = 64
LN_EPS = 1e-5
NEG = -1e30
ROUND = 12582912.0


class Core:
    pass


Residents = namedtuple("Residents", "qT kT v2 segments")
Mask = namedtuple("Mask", "rhs copy", defaults=(None,))
OneHot = namedtuple("OneHot", "top index hot")


class Chain:

    def __init__(self, eng, sem, i=None, per=0):
        self.eng, self.sem, self.i, self.per, self.n = eng, sem, i, per, 0

    def did(self, ins):
        ins.then_inc(self.sem, 1)
        self.n += 1
        return self.n

    def wait(self, n=None):
        n = self.n if n is None else n
        self.eng.wait_ge(self.sem, n if self.i is None else self.per * self.i + n)

    def close(self):
        assert self.i is None or self.per == self.n, f"a round has {self.n} steps, not {self.per}"


def wait(eng, sem, value):
    if not isinstance(value, int) or value > 0:
        eng.wait_ge(sem, value)


def settle(eng, k):
    eng.sem_inc(k.settled, 1)


def pipeline(eng, count, parts, unroll=2, behind=2):
    deepest = max(lag for lag, _ in parts)
    start = deepest + behind
    start += (count - start) % unroll

    def step(n, parity):
        for lag, part in parts:
            if not isinstance(n, int) or 0 <= n - lag < count:
                part(n - lag, (parity - lag) % unroll)

    for n in range(min(start, count)):
        step(n, n % unroll)
    if count > start:
        with eng.Fori(0, (count - start) // unroll) as i:
            for v in range(unroll):
                step(i * unroll + (start + v), (start + v) % unroll)
    for n in range(count, count + deepest):
        step(n, n % unroll)


def rounds(eng, count, steps):
    steps(0)
    with eng.Fori(0, count - 1) as i:
        steps(i + 1)


def upto(value, most):
    return min(value, most) if isinstance(value, int) else value


def sems(nc, ctx, phase, names):
    s = namedtuple("Semaphores", names)(*(nc.alloc_semaphore(f"{phase}_{n}") for n in names.split()))

    def give_back():
        nc.clear_and_free_semaphores(list(s))
        nc.all_engine_barrier()

    ctx.callback(give_back)
    return s



def finish_stats_act(act, k, s):
    act.wait_ge(s.var_ready, 1)
    act.activation(k.rstd[:, :], k.rstd[:, :], ACT.Sqrt).then_inc(s.std_ready, 1)


def finish_stats_dve(dve, k, s):
    dve.tensor_scalar(k.rstd[:, :], k.mv[:, :, 1], LN_EPS, None, ALU.add).then_inc(s.var_ready, 1)
    dve.wait_ge(s.std_ready, 1)
    dve.reciprocal(k.rstd[:, :], k.rstd[:, :]).then_inc(s.rstd_ready, 1)
    dve.wait_ge(s.rstd_ready, 1)


def layernorm(dve, k, h, g):
    for j in range(TG):
        t = TG * g + j
        last = dve.tensor_scalar(h[:, j, :], k.x[:, t, :], k.mv[:, t, 0:1], k.rstd[:, bass.ds(t, 1)],
                                 ALU.subtract, ALU.mult)
    return last


def new_x_dve(dve, k, s, chain, y, g, i, u):
    wait(dve, s.x_done, LANES * i)
    dve.tensor_tensor(k.xn[:, u], k.x[:, bass.ds(TG * g, TG), :], y, ALU.add).then_inc(s.xn_ready, 1)
    dve.wait_ge(s.xn_ready, g + 1)
    xn_stats_dve(dve, k, s, chain, u)


def xn_stats_dve(dve, k, s, chain, u):
    for j in range(TG):
        n = chain.did(dve.bn_stats(k.bn6[:, u, j, :], k.xn[:, u, j, :]))
    chain.wait(n)
    dve.memset(k.pad[:, :], 0.0)
    for j in range(TG):
        last = dve.bn_aggr(k.mvn[:, u, j, :], k.bn6[:, u, j, :])
    last.then_inc(s.stats_ready, 1)


def new_x_pool(pool, k, s, NG):
    def steps(i):
        for u in range(LANES):
            g = LANES * i + u
            pool.wait_ge(s.xn_ready, g + 1)
            settle(pool, k)
            pool.tensor_copy(k.x[:, bass.ds(TG * g, TG), :], k.xn[:, u])
            pool.wait_ge(s.stats_ready, g + 1)
            settle(pool, k)
            pool.tensor_copy(k.mv[:, bass.ds(TG * g, TG), :], k.mvn[:, u]).then_inc(s.x_done, 1)

    rounds(pool, NG // LANES, steps)


def x_update_dve(dve, k, s, g, par, y, tiles=TG):
    wait(dve, s.x_done, g - 1)
    wait(dve, s.xb_ready, g + 1)
    y(k.xn[:, par, 0:tiles])
    dve.wait_ge(s.xn_ready, g + 1)
    stats_of_xn(dve, k, s, g, par, tiles)


def stats_of_xn(dve, k, s, g, par, tiles):
    chain = Chain(dve, s.stats_chain, g, tiles)
    for j in range(tiles):
        n = chain.did(dve.bn_stats(k.bn6[:, par, j, :], k.xn[:, par, j, :]))
    chain.wait(n)
    dve.memset(k.pad[:, :], 0.0)
    for j in range(tiles):
        last = dve.bn_aggr(k.mvn[:, par, j, :], k.bn6[:, par, j, :])
    last.then_inc(s.stats_ready, 1)


def xb_pool(pool, k, s, g, par, row=None, tiles=TG):
    wait(pool, s.xn_ready, g - 1)
    settle(pool, k)
    x = k.x[:, bass.ds(tiles * g, tiles), :]
    if row is None:
        pool.tensor_copy(k.xb[:, par, 0:tiles], x).then_inc(s.xb_ready, 1)
    else:
        pool.tensor_tensor(k.xb[:, par, 0:tiles], x, row[:, :].unsqueeze(1).to_broadcast([P, tiles, D]),
                           ALU.add).then_inc(s.xb_ready, 1)


def x_copy_pool(pool, k, s, g, par, tiles=TG):
    pool.wait_ge(s.xn_ready, g + 1)
    settle(pool, k)
    pool.tensor_copy(k.x[:, bass.ds(tiles * g, tiles), :], k.xn[:, par, 0:tiles])
    pool.wait_ge(s.stats_ready, g + 1)
    settle(pool, k)
    pool.tensor_copy(k.mv[:, bass.ds(tiles * g, tiles), :], k.mvn[:, par, 0:tiles]).then_inc(s.x_done, 1)


def four_transposes(pe, k, out, src):
    for j in range(TG):
        last = pe.transpose(out[:, P * j:P * j + P], src[:, j, :], k.ident[:, :])
    return last


def phase_start(nc, k):
    with ExitStack() as ctx:
        PIECES = 4
        TP = k.NT // PIECES
        s = sems(nc, ctx, "start", "consts x0 x1 x2 x3 stats_ready")
        loaded = (s.x0, s.x1, s.x2, s.x3)
        bn6 = ctx.enter_context(nc.sbuf_tensor("start_bn6", [P, k.NT, 6], F32))
        block = ctx.enter_context(nc.Block())

        @block.sync
        def _(sp):
            x = k.dram["x"].rearrange("(t p) c -> p t c", p=P)
            for n in range(PIECES):
                sp.dma_start(k.x[:, TP * n:TP * n + TP, :], x[:, TP * n:TP * n + TP, :]).then_inc(loaded[n], 16)
            sp.dma_start(k.consts[:, :], k.dram["consts"]).then_inc(s.consts, 16)

        @block.gpsimd
        def _(pool):
            pool.memset(k.pad[:, :], 0.0).then_inc(k.started, 1)

        @block.vector
        def _(dve):
            for n in range(PIECES):
                dve.wait_ge(loaded[n], 16)
                for t in range(TP * n, TP * n + TP):
                    last = dve.bn_stats(bn6[:, t, :], k.x[:, t, :])
                last.then_inc(s.stats_ready, 1)
            dve.wait_ge(s.stats_ready, PIECES)
            dve.wait_ge(k.started, 1)
            dve.memset(k.pad[:, :], 0.0)
            for t in range(k.NT):
                dve.bn_aggr(k.mv[:, t, :], bn6[:, t, :])
            dve.wait_ge(s.consts, 16)
            dve.tensor_copy(k.identb[:, :], k.ident[:, :])
            dve.tensor_copy(k.causalb[:, :], k.causal)
            for j in range(TG):
                dve.tensor_copy(k.causal2b[:, P * j:P * j + P], k.causal2)
                dve.tensor_copy(k.same2b[:, P * j:P * j + P], k.same2)



def phase_l0_attention(nc, k):
    d = k.dram
    with ExitStack() as ctx:
        def sb(name, shape, dt=F32):
            return ctx.enter_context(nc.sbuf_tensor(f"l0a_{name}", shape, dt))

        s = sems(nc, ctx, "l0a", "var_ready std_ready rstd_ready weights ctx_loaded h_ready hT_psum hT_ready q_psum k_psum v_psum "
                 "feat_exp vT_ready qk_ready kq_psum kq_ready o_psum o_ready oT_psum oT_ready y_psum xn_ready stats_ready x_done chain act_chain")
        w = sb("w", [P, 4, D])
        wrow = sb("wrow", [1, 3, GT])
        bv = sb("bv", [P, 1])
        ctxT = sb("ctxT", [P, LANES, GT])
        h = sb("h", [P, LANES, TG, D])
        hT = sb("hT", [P, LANES, GT])
        e = sb("e", [P, LANES, 2, GT])
        r = sb("r", [P, LANES, 2, GT])
        qk = sb("qk", [P, LANES, 2, TG, D])
        prod = sb("prod", [P, LANES, TG, D])
        den = sb("den", [P, LANES, TG * H])
        vT = sb("vT", [P, LANES, GT])
        kq = sb("kq", [P, LANES, SG, D])
        o = sb("o", [P, LANES, TG, D])
        oT = sb("oT", [P, LANES, GT])
        ps = k.psum
        block = ctx.enter_context(nc.Block())

        @block.sync
        def _(sp):
            for n, name in enumerate(("L0_xattn_Wq", "L0_xattn_Wk", "L0_xattn_Wv", "L0_xattn_Wo")):
                sp.dma_start(w[:, n, :], d[name]).then_inc(s.weights, 16)
            for n, name in enumerate(("L0_xattn_bq", "L0_xattn_bk", "L0_xattn_bo")):
                sp.dma_start(wrow[:, n, :], d[name + "_x4"]).then_inc(s.weights, 16)
            sp.dma_start(bv[:, :], d["L0_xattn_bv"]).then_inc(s.weights, 16)
            def steps(i):
                for u in range(LANES):
                    wait(sp, s.v_psum, LANES * i)
                    sp.dma_start(ctxT[:, u, :], d["ctxT"][:, bass.ds((LANES * i + u) * GT, GT)]).then_inc(s.ctx_loaded, 16)

            rounds(sp, k.NG // LANES, steps)

        @block.tensor
        def _(pe):
            pe.wait_ge(s.weights, 16 * 8)
            def steps(i):
                for u in range(LANES):
                    pe.wait_ge(s.h_ready, LANES * i + u + 1)
                    wait(pe, s.oT_ready, LANES * i)
                    four_transposes(pe, k, ps[4 * u], h[:, u]).then_inc(s.hT_psum, 1)
                for u in range(LANES):
                    pe.wait_ge(s.ctx_loaded, 16 * LANES * (i + 1))
                    wait(pe, s.xn_ready, LANES * i)
                    pe.matmul(ps[4 * u + 2][:, :], k.ones[0:1, 0:P], wrow[:, 1, :], start=True, stop=False)
                    for j in range(TG):
                        last = pe.matmul(ps[4 * u + 2][:, D * j:D * j + D], ctxT[:, u, P * j:P * j + P], w[:, 1, :],
                                         start=False, stop=(j == TG - 1))
                    last.then_inc(s.k_psum, 1)
                    pe.matmul(ps[4 * u + 3][:, :], w[:, 2, :], ctxT[:, u, :], start=True, stop=True).then_inc(s.v_psum, 1)
                for u in range(LANES):
                    pe.wait_ge(s.hT_ready, LANES * i + u + 1)
                    pe.matmul(ps[4 * u + 1][:, :], k.ones[0:1, 0:P], wrow[:, 0, :], start=True, stop=False)
                    for j in range(TG):
                        last = pe.matmul(ps[4 * u + 1][:, D * j:D * j + D], hT[:, u, P * j:P * j + P], w[:, 0, :],
                                         start=False, stop=(j == TG - 1))
                    last.then_inc(s.q_psum, 1)
                for u in range(LANES):
                    pe.wait_ge(s.qk_ready, LANES * i + u + 1)
                    for q in range(SG):
                        lo = S * (q % 2)
                        last = pe.matmul(ps[4 * u + 1 + q % 2][:, D * (q // 2):D * (q // 2) + D],
                                         qk[lo:lo + S, u, 1, q // 2, :], qk[lo:lo + S, u, 0, q // 2, :],
                                         start=True, stop=True)
                    last.then_inc(s.kq_psum, 1)
                for u in range(LANES):
                    pe.wait_ge(s.kq_ready, LANES * i + u + 1)
                    pe.wait_ge(s.vT_ready, LANES * i + u + 1)
                    for q in range(SG):
                        lo = S * (q % 2)
                        last = pe.matmul(ps[4 * u + 3][lo:lo + S, D * (q // 2):D * (q // 2) + D],
                                         vT[:, u, S * q:S * q + S], kq[:, u, q, :], start=True, stop=True)
                    last.then_inc(s.o_psum, 1)
                for u in range(LANES):
                    pe.wait_ge(s.o_ready, LANES * i + u + 1)
                    four_transposes(pe, k, ps[4 * u], o[:, u]).then_inc(s.oT_psum, 1)
                for u in range(LANES):
                    pe.wait_ge(s.oT_ready, LANES * i + u + 1)
                    pe.matmul(ps[4 * u + 1][:, :], k.ones[0:1, 0:P], wrow[:, 2, :], start=True, stop=False)
                    for j in range(TG):
                        last = pe.matmul(ps[4 * u + 1][:, D * j:D * j + D], oT[:, u, P * j:P * j + P], w[:, 3, :],
                                         start=False, stop=(j == TG - 1))
                    last.then_inc(s.y_psum, 1)

            rounds(pe, k.NG // LANES, steps)

        @block.gpsimd
        def _(pool):
            new_x_pool(pool, k, s, k.NG)

        @block.scalar
        def _(act):
            finish_stats_act(act, k, s)
            act.wait_ge(s.weights, 16 * 8)
            def steps(i):
                for u in range(LANES):
                    act.wait_ge(s.hT_psum, LANES * i + u + 1)
                    act.copy(hT[:, u, :], ps[4 * u][:, :]).then_inc(s.hT_ready, 1)
                for u in range(LANES):
                    act.wait_ge(s.k_psum, LANES * i + u + 1)
                    wait(act, s.qk_ready, LANES * i)
                    act.activation(e[:, u, 1, :], ps[4 * u + 2][:, :], ACT.Exp)
                    act.activation(r[:, u, 1, :], ps[4 * u + 2][:, :], ACT.Relu)
                    act.wait_ge(s.v_psum, LANES * i + u + 1)
                    wait(act, s.o_psum, LANES * i)
                    act.activation(vT[:, u, :], ps[4 * u + 3][:, :], ACT.Identity, bias=bv[:, 0:1]).then_inc(s.vT_ready, 1)
                for u in range(LANES):
                    act.wait_ge(s.q_psum, LANES * i + u + 1)
                    act.activation(e[:, u, 0, :], ps[4 * u + 1][:, :], ACT.Exp)
                    act.activation(r[:, u, 0, :], ps[4 * u + 1][:, :], ACT.Relu).then_inc(s.feat_exp, 1)
                for u in range(LANES):
                    act.wait_ge(s.oT_psum, LANES * i + u + 1)
                    wait(act, s.y_psum, LANES * i)
                    act.copy(oT[:, u, :], ps[4 * u][:, :]).then_inc(s.oT_ready, 1)

            rounds(act, k.NG // LANES, steps)

        @block.vector
        def _(dve):
            finish_stats_dve(dve, k, s)
            def steps(i):
                chain = Chain(dve, s.chain, i, 16)
                for u in range(LANES):
                    wait(dve, s.hT_psum, LANES * i)
                    layernorm(dve, k, h[:, u], LANES * i + u).then_inc(s.h_ready, 1)
                for u in range(LANES):
                    dve.wait_ge(s.feat_exp, LANES * i + u + 1)
                    wait(dve, s.kq_psum, LANES * i)
                    chain.did(dve.scalar_tensor_tensor(
                        out=qk[:, u].rearrange("p a t c -> p (a t c)"), in0=e[:, u].rearrange("p a n -> p (a n)"), scalar=1.0,
                        in1=r[:, u].rearrange("p a n -> p (a n)"), op0=ALU.min, op1=ALU.add))
                    chain.wait()
                    dve.tensor_tensor(prod[:, u], qk[:, u, 0], qk[:, u, 1], ALU.mult).then_inc(s.qk_ready, 1)
                    dve.wait_ge(s.qk_ready, LANES * i + u + 1)
                    chain.did(dve.tensor_reduce(den[:, u, :], prod[:, u].rearrange("p t (h e) -> p (t h) e", e=HD), AX_X, ALU.add))
                    chain.wait()
                    chain.did(dve.tensor_scalar(den[:, u, :], den[:, u, :], 1e-6, None, ALU.add))
                    chain.wait()
                    chain.did(dve.reciprocal(den[:, u, :], den[:, u, :]))
                for u in range(LANES):
                    dve.wait_ge(s.kq_psum, LANES * i + u + 1)
                    wait(dve, s.o_psum, LANES * i)
                    for b in range(2):
                        last = dve.tensor_tensor(kq[:, u, b::2, :], ps[4 * u + 1 + b].rearrange("p (q c) -> p q c", q=4),
                                                 k.headblock.unsqueeze(1).to_broadcast([P, 4, D]), ALU.mult)
                    last.then_inc(s.kq_ready, 1)
                for u in range(LANES):
                    chain.wait(4 * u + 4)
                    dve.wait_ge(s.o_psum, LANES * i + u + 1)
                    wait(dve, s.oT_psum, LANES * i)
                    dve.tensor_tensor(o[:, u].rearrange("p t (h e) -> p (t h) e", e=HD),
                                      ps[4 * u + 3].rearrange("p (h e) -> p h e", e=HD),
                                      den[:, u, :].unsqueeze(2).to_broadcast([P, TG * H, HD]), ALU.mult).then_inc(s.o_ready, 1)
                for u in range(LANES):
                    dve.wait_ge(s.y_psum, LANES * i + u + 1)
                    new_x_dve(dve, k, s, chain, ps[4 * u + 1].rearrange("p (t c) -> p t c", c=D), LANES * i + u, i, u)
                chain.close()

            rounds(dve, k.NG // LANES, steps)


X_SEMS = "var_ready std_ready rstd_ready xb_ready xn_ready stats_chain stats_ready x_done "



def quantise_rows(dve, chain, q, h, scal, mean):
    amax, r, inv, rec = scal[:, 0, :], scal[:, 1, :], scal[:, INV, :], scal[:, 6, :]
    chain.wait(chain.did(dve.tensor_tensor(amax, amax, r, ALU.mult)))
    chain.wait(chain.did(dve.tensor_scalar(amax, amax, 1e-5, None, ALU.max)))
    chain.did(dve.tensor_scalar(inv, amax, mean, 1.0 / 127.0, ALU.mult, ALU.mult))
    chain.wait(chain.did(dve.reciprocal(rec, amax)))
    chain.wait(chain.did(dve.tensor_scalar(rec, rec, 127.0, None, ALU.mult)))
    for j in range(TG):
        n = chain.did(dve.tensor_scalar(h[:, j, :], h[:, j, :], r[:, j:j + 1], rec[:, j:j + 1], ALU.mult, ALU.mult))
    chain.wait(n)
    chain.wait(chain.did(dve.tensor_scalar(h, h, ROUND, ROUND, ALU.add, ALU.subtract)))
    return dve.tensor_scalar(q, h, 127.0, -128.0, ALU.min, ALU.max)


def phase_l0_ffn(nc, k):
    d = k.dram
    FC = F0 // P
    with ExitStack() as ctx:
        def sb(name, shape, dt=F32):
            return ctx.enter_context(nc.sbuf_tensor(f"l0f_{name}", shape, dt))

        s = sems(nc, ctx, "l0f", X_SEMS + "weights w_chain w_part w_sum w_ready half_ready rms2_mean rms_var rms_std rms_ready a_chain q_ready qT_psum qT_ready "
                 "h_psum h_ready gelu_ready rms2_arg rms2_ready b_chain q2_ready q2T_psum q2T_ready y_psum")
        w1f = sb("w1f", [P, F0])
        w2f = sb("w2f", [P, FC * D])
        w1 = sb("w1", [P, F0], BF16)
        w2 = sb("w2", [P, FC, D], BF16)
        b1 = sb("b1", [P, F0])
        b2 = sb("b2", [P, D])
        wsum = sb("wsum", [P, 6])
        rms = sb("rms", [P, k.NT])
        h = sb("h", [P, TG, D])
        scal1 = sb("scal1", [P, 2, 8, TG])
        scal = sb("scal", [P, 2, 8, TG])
        q = sb("q", [P, 2, TG, D], BF16)
        qT = sb("qT", [P, 2, GT], BF16)
        h2 = sb("h2", [P, 2, TG, F0])
        sq = sb("sq", [P, 2, TG, F0], BF16)
        q2 = sb("q2", [P, 2, TG, F0], BF16)
        q2T = sb("q2T", [P, 2, TG, F0], BF16)
        half = sb("half", [P, TG])
        ps = k.psum
        psb = [p.bitcast(BF16) for p in ps]
        block = ctx.enter_context(nc.Block())

        @block.sync
        def _(sp):
            for dst, name in ((w1f, "L0_ffn_w1T"), (w2f, "L0_ffn_w2T"), (b1, "L0_ffn_b1"), (b2, "L0_ffn_b2")):
                sp.dma_start(dst[:, :], d[name]).then_inc(s.weights, 16)

        @block.tensor
        def _(pe):
            for n in range(2):
                pe.wait_ge(s.w_part, n + 1)
                pe.matmul(ps[n][:, 0:1], k.ones[:, 0:P], wsum[:, n:n + 1], start=True, stop=True).then_inc(s.w_sum, 1)
            pe.wait_ge(s.w_ready, 2)

            def turn_q(g, par):
                pe.wait_ge(s.q_ready, g + 1)
                wait(pe, s.qT_ready, g)
                for j in range(TG):
                    last = pe.transpose(psb[4][:, P * j:P * j + P], q[:, par, j, :], k.identb[:, :])
                last.then_inc(s.qT_psum, 1)

            def up(g, par):
                pe.wait_ge(s.qT_ready, g + 1)
                wait(pe, s.h_ready, g)
                for j in range(TG):
                    last = pe.matmul(ps[j][:, :], qT[:, par, P * j:P * j + P], w1[:, :], start=True, stop=True)
                last.then_inc(s.h_psum, 1)

            def turn_q2(g, par):
                pe.wait_ge(s.q2_ready, g + 1)
                wait(pe, s.q2T_ready, g)
                for j in range(TG):
                    for c in range(FC):
                        at = (j % 2) * F0 + P * c
                        last = pe.transpose(psb[5 + j // 2][:, at:at + P], q2[:, par, j, P * c:P * c + P], k.identb[:, :])
                last.then_inc(s.q2T_psum, 1)

            def down(g, par):
                pe.wait_ge(s.q2T_ready, g + 1)
                wait(pe, s.xn_ready, g)
                for j in range(TG):
                    for c in range(FC):
                        last = pe.matmul(ps[7][:, D * j:D * j + D], q2T[:, par, j, P * c:P * c + P], w2[:, c, :],
                                         start=(c == 0), stop=(c == FC - 1))
                last.then_inc(s.y_psum, 1)

            pipeline(pe, k.NG, [(1, up), (0, turn_q), (3, down), (2, turn_q2)])

        @block.scalar
        def _(act):
            finish_stats_act(act, k, s)
            act.wait_ge(s.rms_var, 1)
            act.activation(rms[:, :], rms[:, :], ACT.Sqrt).then_inc(s.rms_std, 1)

            def copy_qT(g, par):
                act.wait_ge(s.qT_psum, g + 1)
                wait(act, s.h_psum, g - 1)
                act.copy(qT[:, par, :], psb[4][:, 0:GT]).then_inc(s.qT_ready, 1)

            def gelu(g, par):
                act.wait_ge(s.h_ready, g + 1)
                act.activation(h2[:, par].rearrange("p t f -> p (t f)"), h2[:, par].rearrange("p t f -> p (t f)"),
                               ACT.Gelu).then_inc(s.gelu_ready, 1)
                act.wait_ge(s.gelu_ready, g + 1)
                wait(act, s.rms2_ready, g - 1)
                for j in range(TG):
                    last = act.activation(sq[:, par, j, :], h2[:, par, j, :], ACT.Square, scale=float(F0) ** -0.5, accum_out=scal[:, par, 2, j:j + 1])
                last.then_inc(s.rms2_arg, 1)

            def copy_q2T(g, par):
                act.wait_ge(s.q2T_psum, g + 1)
                wait(act, s.y_psum, g - 1)
                for b in range(2):
                    last = act.copy(q2T[:, par, 2 * b:2 * b + 2, :].rearrange("p t f -> p (t f)"), psb[5 + b])
                last.then_inc(s.q2T_ready, 1)

            pipeline(act, k.NG, [(1, gelu), (0, copy_qT), (2, copy_q2T)])

        @block.gpsimd
        def _(pool):
            pool.wait_ge(s.weights, 16 * 4)
            pool.memset(half[:, :], -0.5).then_inc(s.half_ready, 1)
            pool.wait_ge(s.half_ready, 1)

            def rms2(g, par):
                pool.wait_ge(s.rms2_arg, g + 1)
                wait(pool, s.q2_ready, g - 1)
                settle(pool, k)
                pool.tensor_scalar(scal[:, par, 3, :], scal[:, par, 2, :], 1e-5, None, ALU.add).then_inc(s.rms2_mean, 1)
                pool.wait_ge(s.rms2_mean, g + 1)
                pool.tensor_tensor(scal[:, par, 4, :], scal[:, par, 3, :], half[:, :], ALU.pow).then_inc(s.rms2_ready, 1)

            pipeline(pool, k.NG, [(1, rms2), (2, lambda g, par: xb_pool(pool, k, s, g, par, b2)),
                                  (3, lambda g, par: x_copy_pool(pool, k, s, g, par))])

        @block.vector
        def _(dve):
            finish_stats_dve(dve, k, s)
            chain = Chain(dve, s.w_chain)
            chain.wait(chain.did(dve.tensor_tensor(rms[:, :], k.rstd[:, :], k.rstd[:, :], ALU.mult)))
            chain.wait(chain.did(dve.tensor_tensor(rms[:, :], rms[:, :], k.mv[:, :, 1], ALU.mult)))
            dve.tensor_scalar(rms[:, :], rms[:, :], 1e-5, None, ALU.add).then_inc(s.rms_var, 1)
            dve.wait_ge(s.weights, 16 * 4)
            for n, (w, wq, count) in enumerate(((w1f[:, :], w1[:, :], F0 * D), (w2f[:, :], w2[:, :, :].rearrange("p c n -> p (c n)"), F0 * D))):
                dve.tensor_reduce(wsum[:, n:n + 1], w, AX_X, ALU.add, apply_absolute_value=True).then_inc(s.w_part, 1)
                dve.wait_ge(s.w_sum, n + 1)
                mean, inverse = wsum[:, 2 + n:3 + n], wsum[:, 4 + n:5 + n]
                chain.wait(chain.did(dve.tensor_scalar(mean, ps[n][:, 0:1], 1.0 / count, 1e-5, ALU.mult, ALU.max)))
                chain.wait(chain.did(dve.reciprocal(inverse, mean)))
                chain.wait(chain.did(dve.tensor_scalar(w, w, inverse, ROUND, ALU.mult, ALU.add)))
                chain.wait(chain.did(dve.tensor_scalar(w, w, ROUND, 1.0, ALU.subtract, ALU.min)))
                dve.tensor_scalar(wq, w, -1.0, None, ALU.max).then_inc(s.w_ready, 1)
            dve.wait_ge(s.rms_std, 1)
            dve.reciprocal(rms[:, :], rms[:, :]).then_inc(s.rms_ready, 1)
            dve.wait_ge(s.rms_ready, 1)

            def quantise_x(g, par):
                chain = Chain(dve, s.a_chain, g, TG + 12)
                wait(dve, s.q_ready, g)
                for j in range(TG):
                    t = TG * g + j
                    n = chain.did(dve.tensor_scalar(h[:, j, :], k.x[:, bass.ds(t, 1), :], k.mv[:, bass.ds(t, 1), 0], k.rstd[:, bass.ds(t, 1)],
                                                    ALU.subtract, ALU.mult))
                chain.wait(n)
                wait(dve, s.h_ready, g - 1)
                chain.did(dve.tensor_copy(scal1[:, par, 1, :], rms[:, bass.ds(TG * g, TG)]))
                chain.wait(chain.did(dve.tensor_reduce(scal1[:, par, 0, :], h[:, :, :], AX_X, ALU.max, apply_absolute_value=True)))
                wait(dve, s.qT_psum, g - 1)
                quantise_rows(dve, chain, q[:, par], h[:, :, :], scal1[:, par], wsum[:, 2:3]).then_inc(s.q_ready, 1)
                chain.close()

            def bias(g, par):
                dve.wait_ge(s.h_psum, g + 1)
                wait(dve, s.q2_ready, g - 1)
                for j in range(TG):
                    last = dve.scalar_tensor_tensor(out=h2[:, par, j, :], in0=ps[j], scalar=scal1[:, par, INV, j:j + 1], in1=b1[:, :],
                                                    op0=ALU.mult, op1=ALU.add)
                last.then_inc(s.h_ready, 1)

            def quantise_h(g, par):
                chain = Chain(dve, s.b_chain, g, 12)
                dve.wait_ge(s.rms2_arg, g + 1)
                chain.did(dve.tensor_reduce(scal[:, par, 0, :], h2[:, par], AX_X, ALU.max, apply_absolute_value=True))
                dve.wait_ge(s.rms2_ready, g + 1)
                chain.did(dve.tensor_copy(scal[:, par, 1, :], scal[:, par, 4, :]))
                chain.wait()
                wait(dve, s.q2T_psum, g - 1)
                quantise_rows(dve, chain, q2[:, par], h2[:, par], scal[:, par], wsum[:, 3:4]).then_inc(s.q2_ready, 1)
                chain.close()

            def new_x(g, par):
                dve.wait_ge(s.y_psum, g + 1)

                def scaled(xn):
                    for j in range(TG):
                        last = dve.scalar_tensor_tensor(out=xn[:, j, :], in0=ps[7][:, D * j:D * j + D], scalar=scal[:, par, INV, j:j + 1],
                                                        in1=k.xb[:, par, j, :], op0=ALU.mult, op1=ALU.add)
                    last.then_inc(s.xn_ready, 1)

                x_update_dve(dve, k, s, g, par, scaled)

            pipeline(dve, k.NG, [(0, quantise_x), (1, bias), (2, quantise_h), (3, new_x)])



def attention_core(nc, k, name, r, softmax_scale, wo_name, mask=None, bv=None, bo=None):
    with ExitStack() as ctx:
        def sb(n, shape, dt=F32):
            return ctx.enter_context(nc.sbuf_tensor(f"{name}_{n}", shape, dt))

        s = sems(nc, ctx, name, "xb_ready xn_ready stats_chain stats_ready x_done weights cleared q_ready v_ready score_psum max_ready "
                 "centred exp_ready sum_ready rec16_ready rec_ready pT_psum pT_ready o_psum recT_ready o_scaled o_ready y_psum")
        wo = sb("wo", [P, D])
        bias_v = sb("bias_v", [P, 1])
        orow = sb("orow", [P, D])
        kbd = sb("kbd", [P, 2, 2, 4, S])
        qT = sb("qT", [P, 2, P])
        vbd = sb("vbd", [P, 2, 2, H // 2, 32])
        top = sb("top", [P, 2, 16])
        prob = sb("prob", [P, 2, 16, S])
        pT = sb("pT", [P, 2, 8, P])
        total = sb("total", [P, 2, H])
        rec16 = sb("rec16", [P, 2, H])
        rec = sb("rec", [P, 2, D])
        recT = sb("recT", [P, P])
        oT = sb("oT", [P, 2, P])
        ps = k.psum
        block = ctx.enter_context(nc.Block())

        scores = k.banks[:, 0:4, 0:4 * S].rearrange("p a (b n) -> p a b n", n=S)
        oT_psum, recT_psum = ps[6][:, 0:P], ps[6][:, P:2 * P]

        @block.sync
        def _(sp):
            sp.dma_start(wo[:, :], k.dram[wo_name]).then_inc(s.weights, 16)
            sp.dma_start(bias_v[:, :], k.dram[bv or "zero_column"]).then_inc(s.weights, 16)
            sp.dma_start(orow[:, :], k.dram[bo or "zero_row"]).then_inc(s.weights, 16)

        @block.gpsimd
        def _(pool):
            pool.wait_ge(s.weights, 16 * 3)
            pool.memset(vbd[:, :, :, :, :].rearrange("p a b c d -> p (a b c d)"), 0.0).then_inc(s.cleared, 1)
            pool.wait_ge(s.cleared, 1)

            def prepare(t, par):
                if mask and mask.copy:
                    mask.copy(pool, t, par, s.score_psum)
                wait(pool, s.score_psum, 2 * (t - 1))
                settle(pool, k)
                pool.tensor_tensor(kbd[:, par],
                                   r.kT[:, bass.ds(P * t, P)].rearrange("p (b n) -> p b n", b=2).unsqueeze(2).to_broadcast([P, 2, 4, S]),
                                   k.headmask.unsqueeze(1).unsqueeze(3).to_broadcast([P, 2, 4, S]), ALU.mult)
                pool.tensor_copy(qT[:, par], r.qT[:, bass.ds(P * t, P)]).then_inc(s.q_ready, 1)

            def prepare_v(t, par):
                wait(pool, s.o_psum, t - 1)
                wait(pool, s.q_ready, upto(t + 3, k.NT))
                for p in range(2):
                    settle(pool, k)
                    pool.tensor_copy(
                        vbd[64 * p:64 * p + 64, par].rearrange("p b (a e) (f n) -> p (b a) (e f) n", e=2, f=2)[:, :, 0:4:3, HD * p:HD * p + HD],
                        r.v2[64 * p:64 * p + 64, bass.ds(2 * t, 2), :].rearrange("p b (a e n) -> p (b a) e n", e=2, n=HD)
                    ).then_inc(s.v_ready, 1)
                    pool.wait_ge(s.v_ready, 2 * t + 1 + p)

            pipeline(pool, k.NT, [(5, lambda t, par: x_copy_pool(pool, k, s, t, par, 1)),
                                  (3, lambda t, par: xb_pool(pool, k, s, t, par, orow, 1)),
                                  (0, prepare), (2, prepare_v)])

        @block.tensor
        def _(pe):
            pe.wait_ge(s.weights, 16 * 3)

            def score(t, par):
                pe.wait_ge(s.q_ready, t + 1)
                for a in range(4):
                    lo = 32 * a
                    if a % 2 == 0:
                        wait(pe, s.centred, 2 * t - 1 + a // 2)
                    if mask:
                        pe.matmul(scores[:, a], k.identb[:, :], mask.rhs(pe, t, par), start=True, stop=False,
                                  skip_group_check=True)
                    for b in range(2):
                        last = pe.matmul(scores[S * b:S * b + S, a].rearrange("p h n -> p (h n)"),
                                         qT[lo:lo + 32, par, S * b:S * b + S],
                                         kbd[lo:lo + 32, par, b].rearrange("p h n -> p (h n)"), start=not mask, stop=True,
                                         skip_group_check=True)
                    if a % 2:
                        last.then_inc(s.score_psum, 1)

            def turn(t, par):
                pe.wait_ge(s.exp_ready, t + 1)
                wait(pe, s.pT_ready, t)
                for n in range(8):
                    last = pe.transpose(ps[4 + n // 4][:, P * (n % 4):P * (n % 4) + P],
                                        prob[:, par, 2 * n:2 * n + 2, :], k.ident[:, :])
                last.then_inc(s.pT_psum, 1)

            def weigh(t, par):
                pe.wait_ge(s.pT_ready, t + 1)
                pe.wait_ge(s.v_ready, 2 * t + 2)
                wait(pe, s.o_scaled, t)
                for b in range(2):
                    for a in range(4):
                        for j in range(2):
                            pe.matmul(oT_psum[32 * a:32 * a + 32, S * b:S * b + S], vbd[:, par, b, 2 * a + j, :],
                                      pT[:, par, 2 * a + j, S * b:S * b + S], start=(j == 0), stop=(j == 1), skip_group_check=True)
                pe.wait_ge(s.rec_ready, t + 1)
                pe.transpose(recT_psum, rec[:, par], k.ident[:, :]).then_inc(s.o_psum, 1)

            def project(t, par):
                pe.wait_ge(s.o_ready, t + 1)
                wait(pe, s.xn_ready, t)
                pe.matmul(ps[7][:, 0:D], oT[:, par], wo[:, :], start=True, stop=True)\
                    .then_inc(s.y_psum, 1)

            pipeline(pe, k.NT, [(1, score), (2, turn), (4, project), (3, weigh)])

        @block.scalar
        def _(act):
            def copy_pT(t, par):
                act.wait_ge(s.pT_psum, t + 1)
                wait(act, s.o_psum, t - 1)
                act.copy(pT[:, par].rearrange("p a n -> p (a n)"), k.banks[:, 4:6, :].rearrange("p a n -> p (a n)")).then_inc(s.pT_ready, 1)

            def exp(t, par):
                act.wait_ge(s.centred, 2 * t + 2)
                all_heads = prob[:, par].rearrange("p a n -> p (a n)")
                act.activation(all_heads, all_heads, ACT.Exp, scale=softmax_scale).then_inc(s.exp_ready, 1)

            pipeline(act, k.NT, [(2, copy_pT), (1, exp)])

        @block.vector
        def _(dve):
            dve.wait_ge(s.weights, 16 * 3)

            def centre(t, par):
                wait(dve, s.centred, 2 * (t - 1))
                for i in range(2):
                    banks, heads = slice(2 * i, 2 * i + 2), slice(8 * i, 8 * i + 8)
                    dve.wait_ge(s.score_psum, 2 * t + 1 + i)
                    dve.tensor_reduce(top[:, par, heads], scores[:, banks], AX_X, ALU.max).then_inc(s.max_ready, 1)
                    dve.wait_ge(s.max_ready, 2 * t + 1 + i)
                    if i == 0:
                        wait(dve, s.pT_psum, t - 1)
                        wait(dve, s.sum_ready, t - 1)
                    dve.tensor_tensor(prob[:, par, heads].rearrange("p (a b) n -> p a b n", a=2), scores[:, banks],
                                      top[:, par, heads].rearrange("p (a b) -> p a b", a=2).unsqueeze(3).to_broadcast([P, 2, 4, S]),
                                      ALU.subtract).then_inc(s.centred, 1)

            def reciprocals(t, par):
                dve.wait_ge(s.exp_ready, t + 1)
                wait(dve, s.rec16_ready, t - 1)
                dve.tensor_reduce(total[:, par], prob[:, par], AX_X, ALU.add).then_inc(s.sum_ready, 1)
                dve.wait_ge(s.sum_ready, t + 1)
                wait(dve, s.rec_ready, t - 1)
                dve.reciprocal(rec16[:, par], total[:, par]).then_inc(s.rec16_ready, 1)
                dve.wait_ge(s.rec16_ready, t + 1)
                wait(dve, s.o_psum, t - 1)
                dve.tensor_copy(rec[:, par].rearrange("p (h e) -> p h e", e=HD),
                                rec16[:, par].unsqueeze(2).to_broadcast([P, H, HD])).then_inc(s.rec_ready, 1)

            def normalise(t, par):
                dve.wait_ge(s.o_psum, t + 1)
                wait(dve, s.y_psum, t - 1)
                wait(dve, s.o_scaled, t)
                dve.tensor_copy(recT[:, :], recT_psum).then_inc(s.recT_ready, 1)
                dve.wait_ge(s.recT_ready, t + 1)
                dve.tensor_tensor(oT[:, par], oT_psum, recT[:, :], ALU.mult).then_inc(s.o_scaled, 1)
                dve.wait_ge(s.o_scaled, t + 1)
                dve.tensor_scalar(oT[:, par], oT[:, par], bias_v[:, 0:1], None, ALU.add).then_inc(s.o_ready, 1)

            def new_x(t, par):
                dve.wait_ge(s.y_psum, t + 1)

                def add(xn):
                    dve.tensor_tensor(xn[:, 0], k.xb[:, par, 0], ps[7][:, 0:D], ALU.add)\
                        .then_inc(s.xn_ready, 1)

                x_update_dve(dve, k, s, t, par, add, 1)

            parts = [(2, reciprocals), (1, centre), (4, new_x), (3, normalise)]
            pipeline(dve, k.NT, parts)


def residents(nc, k, ctx, name, segments=None):
    return Residents(
        qT=ctx.enter_context(nc.sbuf_tensor(f"{name}_qT", [P, k.NT * P], F32)),
        kT=ctx.enter_context(nc.sbuf_tensor(f"{name}_kT", [P, k.NT * P], F32)),
        v2=ctx.enter_context(nc.sbuf_tensor(f"{name}_v2", [P, 2 * k.NT, D // 2], F32)),
        segments=segments and ctx.enter_context(nc.sbuf_tensor(f"{name}_segments", [P, k.NT], F32)))



def store_v2(dve, k, r, g):
    for p in range(2):
        half = slice(64 * p, 64 * p + 64)
        last = dve.tensor_scalar(r.v2[half, bass.ds(SG * g, SG), :].rearrange("k q (j n) -> k (q j) n", n=HD),
                                 k.banks[half, 6:8, :].rearrange("k b (j n) -> k (b j) n", n=2 * HD)[:, :, HD * p:HD * p + HD],
                                 0.0, None, ALU.add)
    return last


def l1_projections(nc, k, r):
    with ExitStack() as ctx:
        def sb(name, shape, dt=F32):
            return ctx.enter_context(nc.sbuf_tensor(f"l1p_{name}", shape, dt))

        s = sems(nc, ctx, "l1p", "var_ready std_ready rstd_ready weights ctx_loaded h_ready hT_psum hT_ready k_psum k_ready v_psum v_ready q_psum q_ready")
        w = sb("w", [P, 3, D])
        bqk = sb("bqk", [P, 2])
        ctx2 = sb("ctx2", [P, 2, SG, 2, S])
        h = sb("h", [P, 2, TG, D])
        hT = sb("hT", [P, 2, GT])
        ps = k.psum
        block = ctx.enter_context(nc.Block())

        @block.sync
        def _(sp):
            for n, name in enumerate("qkv"):
                sp.dma_start(w[:, n, :], k.dram[f"L1_xattn_W{name}T"]).then_inc(s.weights, 16)
            for n, name in enumerate("qk"):
                sp.dma_start(bqk[:, n:n + 1], k.dram[f"L1_xattn_b{name}"]).then_inc(s.weights, 16)

            def load(g, par):
                wait(sp, s.v_psum, g - 1)
                wait(sp, s.ctx_loaded, 32 * g)
                for copy in range(2):
                    sp.dma_start(ctx2[:, par, :, copy, :], k.dram["ctxT"][:, bass.ds(g * GT, GT)].rearrange("c (q n) -> c q n", n=S))\
                        .then_inc(s.ctx_loaded, 16)

            pipeline(sp, k.NG, [(0, load)])

        @block.tensor
        def _(pe):
            pe.wait_ge(s.weights, 16 * 5)

            def turn(g, par):
                pe.wait_ge(s.h_ready, g + 1)
                wait(pe, s.hT_ready, g - 1)
                four_transposes(pe, k, ps[par], h[:, par]).then_inc(s.hT_psum, 1)

            def keys(g, par):
                pe.wait_ge(s.ctx_loaded, 32 * (g + 1))
                wait(pe, s.k_ready, g - 1)
                pe.matmul(ps[4 + par][:, :], w[:, 1, :], ctx2[:, par, :, 0, :], start=True, stop=True).then_inc(s.k_psum, 1)
                wait(pe, s.v_ready, g)
                for q in range(SG):
                    last = pe.matmul(ps[6 + q // 4][:, D * (q % 4):D * (q % 4) + D], ctx2[:, par, q], w[:, 2, :],
                                     start=True, stop=True)
                last.then_inc(s.v_psum, 1)

            def queries(g, par):
                pe.wait_ge(s.hT_ready, g + 1)
                wait(pe, s.q_ready, g - 1)
                pe.matmul(ps[2 + par][:, :], w[:, 0, :], hT[:, par, :], start=True, stop=True).then_inc(s.q_psum, 1)

            pipeline(pe, k.NG, [(0, turn), (0, keys), (1, queries)])

        @block.scalar
        def _(act):
            finish_stats_act(act, k, s)
            act.wait_ge(s.weights, 16 * 5)

            def copy_hT(g, par):
                act.wait_ge(s.hT_psum, g + 1)
                wait(act, s.q_psum, g - 1)
                act.copy(hT[:, par, :], ps[par]).then_inc(s.hT_ready, 1)

            def store_k(g, par):
                act.wait_ge(s.k_psum, g + 1)
                settle(act, k)
                act.activation(r.kT[:, bass.ds(GT * g, GT)], ps[4 + par], ACT.Identity, bias=bqk[:, 1:2]).then_inc(s.k_ready, 1)

            def store_q(g, par):
                act.wait_ge(s.q_psum, g + 1)
                settle(act, k)
                act.activation(r.qT[:, bass.ds(GT * g, GT)], ps[2 + par], ACT.Identity, bias=bqk[:, 0:1]).then_inc(s.q_ready, 1)

            pipeline(act, k.NG, [(0, copy_hT), (0, store_k), (1, store_q)])

        @block.vector
        def _(dve):
            finish_stats_dve(dve, k, s)

            def norm(g, par):
                wait(dve, s.hT_psum, g - 1)
                layernorm(dve, k, h[:, par], g).then_inc(s.h_ready, 1)

            def store_v(g, par):
                dve.wait_ge(s.v_psum, g + 1)
                store_v2(dve, k, r, g).then_inc(s.v_ready, 1)

            pipeline(dve, k.NG, [(0, norm), (0, store_v)])


def phase_l1_attention(nc, k):
    with ExitStack() as ctx:
        r = residents(nc, k, ctx, "l1")
        l1_projections(nc, k, r)
        mask = Mask(rhs=lambda pe, t, par: k.causalb[:, :])
        attention_core(nc, k, "l1a", r, float(HD) ** -0.5, "L1_xattn_WoT", mask, "L1_xattn_bv", "L1_xattn_bo")



def first_max(dve, chain, z, count, w):
    shape = [P, z.shape[1], z.shape[2]]
    chain.wait(chain.did(dve.tensor_reduce(w.top, z, AX_X, ALU.max)))
    chain.wait(chain.did(dve.tensor_tensor(w.hot, z, w.top.unsqueeze(2).to_broadcast(shape), ALU.is_equal)))
    chain.wait(chain.did(dve.tensor_tensor(w.hot, w.hot, count.unsqueeze(1).to_broadcast(shape), ALU.mult)))
    chain.wait(chain.did(dve.tensor_reduce(w.index, w.hot, AX_X, ALU.min)))
    chain.wait(chain.did(dve.tensor_tensor(w.hot, count.unsqueeze(1).to_broadcast(shape),
                                           w.index.unsqueeze(2).to_broadcast(shape), ALU.is_equal)))


def phase_l1_ffn(nc, k):
    E = 16
    PARTS = 3
    with ExitStack() as ctx:
        def sb(name, shape, dt=F32):
            return ctx.enter_context(nc.sbuf_tensor(f"l1f_{name}", shape, dt))

        s = sems(nc, ctx, "l1f", X_SEMS + "weights w_chain sim_sums sim_root sigmoid norm_var norm_std h_ready hT_psum hT_ready "
                 "logit_psum g_chain gate_exp shift_ready rw_ready rwT_psum rwT_ready qshare_psum xe_ready qkv_psum q_copied v_copied "
                 "score_psum c_chain c_ready exp_ready p_ready pT_psum pT_ready ao_psum ao_ready oshare_psum ae_ready y_psum yT_ready yt_psum")
        w = sb("w", [P, 4, E, D])
        sim = sb("sim", [P, 3, E])
        gates = sb("gates", [P, E])
        sel = sb("sel", [P, E, P], BF16)
        self32 = sb("self32", [P, E, P])
        rnorm = sb("rnorm", [P, k.NT])
        h = sb("h", [P, TG, D])
        hT = sb("hT", [P, 4, GT])
        z = sb("z", [P, TG, E])
        gw = sb("gw", [P, 8, TG, E])
        g1 = sb("g1", [P, 8, TG])
        rw3 = sb("rw3", [P, TG, PARTS, 32], BF16)
        rw3T = sb("rw3T", [32 * PARTS, 4, GT], BF16)
        xe = sb("xe", [P, 2, GT])
        ae = sb("ae", [P, 2, GT])
        qT = sb("qT", [P, GT])
        kT = sb("kT", [P, GT])
        v = sb("v", [P, 2, TG, D])
        prob = sb("prob", [P, TG, P])
        c1 = sb("c1", [P, 3, TG])
        pT = sb("pT", [P, TG, P])
        aoT = sb("aoT", [P, 2, GT])
        yT = sb("yT", [P, TG, P])
        ps = k.psum
        psb0 = ps[0].bitcast(BF16)
        block = ctx.enter_context(nc.Block())
        first_top, first_index, count_top, rec, second_top = range(5)

        @block.sync
        def _(sp):
            for n, name in enumerate("qkvo"):
                sp.dma_start(w[:, n], k.dram[f"L1_ffn_{name}_proj"]).then_inc(s.weights, 16)
            sp.dma_start(sim[:, 0, :], k.dram["L1_ffn_sim_matrix"]).then_inc(s.weights, 16)
            sp.dma_start(gates[:, :], k.dram["L1_ffn_gates"]).then_inc(s.weights, 16)
            sp.dma_start(self32[:, :, :].rearrange("p e n -> p (e n)"), k.dram["selector"]).then_inc(s.weights, 16)

        @block.gpsimd
        def _(pool):
            pipeline(pool, k.NG, [(2, lambda g, m: xb_pool(pool, k, s, g, m % 2)),
                                  (3, lambda g, m: x_copy_pool(pool, k, s, g, m % 2))], unroll=4)

        @block.tensor
        def _(pe):
            pe.wait_ge(s.weights, 16 * 7)
            pe.wait_ge(s.w_chain, 1)
            pe.matmul(ps[0][:, 0:E], k.ones, sim[:, 1, :], start=True, stop=True).then_inc(s.sim_sums, 1)

            def turn(g, m):
                pe.wait_ge(s.h_ready, g + 1)
                wait(pe, s.xn_ready, g - 3)
                wait(pe, s.rwT_ready, g)
                four_transposes(pe, k, ps[0], h).then_inc(s.hT_psum, 1)

            def logits(g, m):
                pe.wait_ge(s.hT_ready, g + 1)
                for j in range(TG):
                    last = pe.matmul(ps[0][:, E * j:E * j + E], hT[:, m, P * j:P * j + P], sim[:, 2, :], start=True, stop=True)
                last.then_inc(s.logit_psum, 1)

            def turn_rw(g, m):
                pe.wait_ge(s.rw_ready, g + 1)
                for j in range(TG):
                    last = pe.transpose(psb0[0:32 * PARTS, P * j:P * j + P], rw3[:, j].rearrange("p a b -> p (a b)"), k.identb[:, :])
                last.then_inc(s.rwT_psum, 1)

            def share(e, m, sem):
                pe.matmul(ps[2 + e % 2], sel[0:32 * PARTS, e, :], rw3T[:, m, :], start=True, stop=True).then_inc(sem, 1)

            def qkv(g, m):
                pe.wait_ge(s.rwT_ready, g + 1)
                wait(pe, s.ae_ready, E * (g - 2))
                share(0, m, s.qshare_psum)
                for e in range(E):
                    if e + 1 < E:
                        wait(pe, s.xe_ready, E * g + e)
                        share(e + 1, m, s.qshare_psum)
                    pe.wait_ge(s.xe_ready, E * g + e + 1)
                    if e == 0:
                        wait(pe, s.q_copied, g)
                        wait(pe, s.v_copied, g)
                    for n in range(2):
                        pe.matmul(ps[4 + n], w[:, n, e, :], xe[:, e % 2, :], start=(e == 0), stop=(e == E - 1))
                    for j in range(TG):
                        last = pe.matmul(ps[6][:, D * j:D * j + D], xe[:, e % 2, P * j:P * j + P], w[:, 2, e, :],
                                         start=(e == 0 and j == 0), stop=(e == E - 1), skip_group_check=True)
                    last.then_inc(s.qkv_psum, 1)

            def score(g, m):
                pe.wait_ge(s.q_copied, g + 1)
                wait(pe, s.ao_ready, g)
                pe.matmul(ps[1], k.identb[:, :], k.causal2b[:, :], start=True, stop=False, skip_group_check=True)
                for j in range(TG):
                    last = pe.matmul(ps[1][:, P * j:P * j + P], qT[:, P * j:P * j + P], kT[:, P * j:P * j + P],
                                     start=False, stop=True, skip_group_check=True)
                last.then_inc(s.score_psum, 1)

            def turn_p(g, m):
                pe.wait_ge(s.p_ready, g + 1)
                four_transposes(pe, k, ps[1], prob).then_inc(s.pT_psum, 1)

            def weigh(g, m):
                pe.wait_ge(s.pT_ready, g + 1)
                pe.wait_ge(s.v_copied, g + 1)
                for j in range(TG):
                    last = pe.matmul(ps[1][:, P * j:P * j + P], v[:, m % 2, j, :], pT[:, j, :], start=True, stop=True)
                last.then_inc(s.ao_psum, 1)

            def out(g, m):
                pe.wait_ge(s.ao_ready, g + 1)
                share(0, m, s.oshare_psum)
                for e in range(E):
                    if e + 1 < E:
                        wait(pe, s.ae_ready, E * g + e)
                        share(e + 1, m, s.oshare_psum)
                    pe.wait_ge(s.ae_ready, E * g + e + 1)
                    if e == 0:
                        wait(pe, s.yT_ready, g)
                    last = pe.matmul(ps[7], w[:, 3, e, :], ae[:, e % 2, :], start=(e == 0), stop=(e == E - 1))
                    last.then_inc(s.y_psum, 1)

            def turn_y(g, m):
                pe.wait_ge(s.yT_ready, g + 1)
                pe.wait_ge(s.rwT_ready, upto(g + 4, k.NG))
                four_transposes(pe, k, ps[0], yT).then_inc(s.yt_psum, 1)

            pipeline(pe, k.NG, [(0, turn), (2, score), (0, logits), (1, qkv), (0, turn_rw), (2, turn_p), (3, out), (2, weigh),
                                (3, turn_y)], unroll=4)

        @block.scalar
        def _(act):
            finish_stats_act(act, k, s)
            act.wait_ge(s.norm_var, 1)
            act.activation(rnorm[:, :], rnorm[:, :], ACT.Sqrt).then_inc(s.norm_std, 1)
            act.wait_ge(s.sim_sums, 1)
            act.activation(sim[:, 1, :], ps[0][:, 0:E], ACT.Sqrt).then_inc(s.sim_root, 1)
            act.activation(gates[:, :], gates[:, :], ACT.Sigmoid).then_inc(s.sigmoid, 1)

            def copy_hT(g, m):
                act.wait_ge(s.hT_psum, g + 1)
                act.copy(hT[:, m, :], ps[0]).then_inc(s.hT_ready, 1)

            def copy_rwT(g, m):
                act.wait_ge(s.rwT_psum, g + 1)
                act.copy(rw3T[:, m, :], psb0[0:32 * PARTS, 0:GT]).then_inc(s.rwT_ready, 1)

            def gate_exp(g, m):
                act.wait_ge(s.shift_ready, g + 1)
                act.activation(gw[:, 0].rearrange("p t e -> p (t e)"), gw[:, 0].rearrange("p t e -> p (t e)"), ACT.Exp)\
                    .then_inc(s.gate_exp, 1)

            def copy_qkv(g, m):
                act.wait_ge(s.qkv_psum, E * (g + 1))
                wait(act, s.score_psum, g)
                act.copy(qT[:, :], ps[4])
                act.copy(kT[:, :], ps[5]).then_inc(s.q_copied, 1)
                wait(act, s.ao_psum, g - 1)
                act.copy(v[:, m % 2].rearrange("p t c -> p (t c)"), ps[6]).then_inc(s.v_copied, 1)

            def exp(g, m):
                act.wait_ge(s.c_ready, g + 1)
                act.activation(prob[:, :, :], prob[:, :, :], ACT.Exp, scale=float(D) ** -0.5).then_inc(s.exp_ready, 1)

            def copy_pT(g, m):
                act.wait_ge(s.pT_psum, g + 1)
                act.copy(pT[:, :, :].rearrange("p t n -> p (t n)"), ps[1]).then_inc(s.pT_ready, 1)

            def copy_ao(g, m):
                act.wait_ge(s.ao_psum, g + 1)
                wait(act, s.ae_ready, E * (g - 1))
                act.copy(aoT[:, m % 2, :], ps[1]).then_inc(s.ao_ready, 1)

            def copy_yT(g, m):
                act.wait_ge(s.y_psum, E * (g + 1))
                wait(act, s.yt_psum, g)
                act.copy(yT[:, :, :].rearrange("p t n -> p (t n)"), ps[7]).then_inc(s.yT_ready, 1)

            pipeline(act, k.NG, [(0, copy_hT), (2, exp), (0, gate_exp), (1, copy_qkv), (0, copy_rwT), (2, copy_pT), (3, copy_yT),
                                 (2, copy_ao)], unroll=4)

        @block.vector
        def _(dve):
            finish_stats_dve(dve, k, s)
            chain = Chain(dve, s.w_chain)
            dve.wait_ge(s.weights, 16 * 7)
            chain.wait(chain.did(dve.tensor_tensor(sim[:, 1, :], sim[:, 0, :], sim[:, 0, :], ALU.mult)))
            chain.wait(chain.did(dve.tensor_tensor(rnorm[:, :], k.rstd[:, :], k.rstd[:, :], ALU.mult)))
            chain.wait(chain.did(dve.tensor_tensor(rnorm[:, :], rnorm[:, :], k.mv[:, :, 1], ALU.mult)))
            dve.tensor_scalar(rnorm[:, :], rnorm[:, :], float(D), 1e-12, ALU.mult, ALU.add).then_inc(s.norm_var, 1)
            dve.wait_ge(s.sim_root, 1)
            chain.wait(chain.did(dve.reciprocal(sim[:, 1, :], sim[:, 1, :])))
            chain.did(dve.tensor_tensor(sim[:, 2, :], sim[:, 0, :], sim[:, 1, :], ALU.mult))
            chain.did(dve.tensor_copy(sel[:, :, :], self32[:, :, :]))
            chain.did(dve.memset(rw3[:, :, :, :].rearrange("p a b c -> p (a b c)"), 0.0))
            dve.wait_ge(s.norm_std, 1)
            chain.did(dve.reciprocal(rnorm[:, :], rnorm[:, :]))
            chain.wait()
            dve.wait_ge(s.sigmoid, 1)

            def norm(g, m):
                wait(dve, s.hT_psum, g)
                layernorm(dve, k, h, g).then_inc(s.h_ready, 1)

            def gate(g, chain, part):
                go = lambda ins: chain.wait(chain.did(ins))
                wide = lambda ap: ap.unsqueeze(2).to_broadcast([P, TG, E])
                every = lambda ap: ap.unsqueeze(1).to_broadcast([P, TG, E])
                W = lambda n: gw[:, n]
                V = lambda n: g1[:, n, :]
                if part == 0:
                    dve.wait_ge(s.logit_psum, g + 1)
                    wait(dve, s.rwT_psum, g)
                    go(dve.tensor_tensor(z[:, :, :], ps[0][:, 0:TG * E].rearrange("p (t e) -> p t e", e=E),
                                         wide(rnorm[:, bass.ds(TG * g, TG)]), ALU.mult))
                    go(dve.tensor_tensor(z[:, :, :], z[:, :, :], every(gates[:, :]), ALU.subtract))
                elif part == 1:
                    one = OneHot(top=V(0), index=V(1), hot=W(1))
                    first_max(dve, chain, z[:, :, :], k.count16, one)
                elif part == 2:
                    go(dve.scalar_tensor_tensor(out=W(3), in0=W(1), scalar=NEG, in1=z[:, :, :], op0=ALU.mult, op1=ALU.add))
                    first_max(dve, chain, W(3), k.count16, OneHot(top=V(2), index=V(3), hot=W(2)))
                elif part == 3:
                    chain.did(dve.tensor_tensor(W(1), W(1), W(2), ALU.add))
                    chain.did(dve.tensor_scalar(W(0), z[:, :, :], 0.0, None, ALU.max))
                    go(dve.tensor_scalar(W(4), z[:, :, :], 0.0, None, ALU.is_gt))
                    chain.did(dve.tensor_scalar(V(0), V(0), 0.0, None, ALU.max))
                    go(dve.tensor_reduce(V(4), W(4), AX_X, ALU.add))
                    go(dve.tensor_scalar(V(4), V(4), 0.0, None, ALU.is_equal))
                    dve.tensor_tensor(W(0), W(0), wide(V(0)), ALU.subtract).then_inc(s.shift_ready, 1)
                elif part == 4:
                    go(dve.tensor_tensor(W(1), W(1), wide(V(4)), ALU.mult))
                    go(dve.tensor_tensor(W(4), W(4), W(1), ALU.add))
                elif part == 5:
                    dve.wait_ge(s.gate_exp, g + 1)
                    go(dve.tensor_tensor(W(0), W(0), W(4), ALU.mult))
                    go(dve.tensor_reduce(V(5), W(0), AX_X, ALU.add))
                    go(dve.reciprocal(V(5), V(5)))
                    go(dve.tensor_tensor(W(5), W(0), wide(V(5)), ALU.mult))
                elif part == 6:
                    go(dve.tensor_copy(rw3[:, :, 0, 0:E], W(5)))
                    go(dve.tensor_tensor(W(6), W(5), rw3[:, :, 0, 0:E], ALU.subtract))
                    go(dve.tensor_copy(rw3[:, :, 1, 0:E], W(6)))
                    go(dve.tensor_tensor(W(7), W(6), rw3[:, :, 1, 0:E], ALU.subtract))
                    dve.tensor_copy(rw3[:, :, 2, 0:E], W(7)).then_inc(s.rw_ready, 1)
                    chain.close()

            def first_gate(g, m):
                if isinstance(g, int) and g == 0:
                    chain = Chain(dve, s.g_chain, g, 29)
                    for part in range(7):
                        gate(g, chain, part)

            def weigh_x(g, m):
                chain = Chain(dve, s.g_chain, g + 1, 29)
                for e in range(E):
                    dve.wait_ge(s.qshare_psum, E * g + e + 1)
                    wait(dve, s.qkv_psum, E * g + e - 1)
                    dve.tensor_tensor(xe[:, e % 2, :], hT[:, m, :], ps[2 + e % 2], ALU.mult).then_inc(s.xe_ready, 1)
                    if e % 2 == 0 and e < 14 and (not isinstance(g, int) or g + 1 < k.NG):
                        gate(g + 1, chain, e // 2)

            def centre(g, m):
                dve.wait_ge(s.score_psum, g + 1)
                sc = ps[1].rearrange("p (t n) -> p t n", n=P)
                dve.tensor_reduce(c1[:, 0, :], sc, AX_X, ALU.max).then_inc(s.c_chain, 1)
                dve.wait_ge(s.c_chain, 3 * g + 1)
                dve.tensor_tensor(prob[:, :, :], sc, c1[:, 0, :].unsqueeze(2).to_broadcast([P, TG, P]), ALU.subtract)\
                    .then_inc(s.c_ready, 1)

            def normalise(g, m):
                dve.wait_ge(s.exp_ready, g + 1)
                dve.tensor_reduce(c1[:, 1, :], prob[:, :, :], AX_X, ALU.add).then_inc(s.c_chain, 1)
                dve.wait_ge(s.c_chain, 3 * g + 2)
                dve.reciprocal(c1[:, 2, :], c1[:, 1, :]).then_inc(s.c_chain, 1)
                dve.wait_ge(s.c_chain, 3 * g + 3)
                dve.tensor_tensor(prob[:, :, :], prob[:, :, :], c1[:, 2, :].unsqueeze(2).to_broadcast([P, TG, P]), ALU.mult)\
                    .then_inc(s.p_ready, 1)

            def weigh_ao(g, m):
                for e in range(E):
                    dve.wait_ge(s.oshare_psum, E * g + e + 1)
                    wait(dve, s.y_psum, E * g + e - 1)
                    dve.tensor_tensor(ae[:, e % 2, :], aoT[:, m % 2, :], ps[2 + e % 2], ALU.mult).then_inc(s.ae_ready, 1)

            def new_x(g, m):
                dve.wait_ge(s.yt_psum, g + 1)

                def add(xn):
                    dve.tensor_tensor(xn, k.xb[:, m % 2], ps[0].rearrange("p (t c) -> p t c", c=D), ALU.add).then_inc(s.xn_ready, 1)

                x_update_dve(dve, k, s, g, m % 2, add)

            pipeline(dve, k.NG, [(0, norm), (2, centre), (0, first_gate), (1, weigh_x), (2, normalise), (3, weigh_ao), (3, new_x)], unroll=4)



def l2_projections(nc, k, r):
    with ExitStack() as ctx:
        def sb(name, shape, dt=F32):
            return ctx.enter_context(nc.sbuf_tensor(f"l2p_{name}", shape, dt))

        s = sems(nc, ctx, "l2p", "var_ready std_ready rstd_ready weights ctx_loaded h_ready hT_psum hT_ready q_psum q_stored score_psum "
                 "hot_chain hot_ready kvw_psum kvw_ready hotT_psum hotT_ready k_psum k_stored v_psum v_stored")
        wq = sb("wq", [P, D])
        wkv = sb("wkv", [P, 2 * D])
        ctxT = sb("ctxT", [P, 4, GT])
        h = sb("h", [P, TG, D])
        hT = sb("hT", [P, 2, GT])
        q = sb("q", [P, 2, GT])
        kvw = sb("kvw", [P, 2, TG, 2 * D])
        hot = sb("hot", [P, TG, P])
        top = sb("top", [P, 2, TG])
        hotT = sb("hotT", [P, SG, 2, S])
        ps = k.psum
        block = ctx.enter_context(nc.Block())

        @block.sync
        def _(sp):
            sp.dma_start(wq[:, :], k.dram["L2_xattn_WqT"]).then_inc(s.weights, 16)
            sp.dma_start(wkv[:, :], k.dram["L2_xattn_WkvT_heads"]).then_inc(s.weights, 16)

            def load(g, m):
                wait(sp, s.kvw_psum, g - 3)
                wait(sp, s.ctx_loaded, 16 * g)
                sp.dma_start(ctxT[:, m, :], k.dram["ctxT"][:, bass.ds(g * GT, GT)]).then_inc(s.ctx_loaded, 16)

            pipeline(sp, k.NG, [(1, load)], unroll=4, behind=4)

        @block.tensor
        def _(pe):
            pe.wait_ge(s.weights, 16 * 2)

            def turn(g, m):
                pe.wait_ge(s.h_ready, g + 1)
                wait(pe, s.hT_ready, g)
                four_transposes(pe, k, ps[0], h).then_inc(s.hT_psum, 1)

            def keys(g, m):
                pe.wait_ge(s.hotT_ready, g + 1)
                pe.wait_ge(s.kvw_ready, g + 1)
                pe.wait_ge(s.q_stored, upto(g + 3, k.NG))
                wait(pe, s.k_stored, g)
                for j in range(TG):
                    last = pe.matmul(ps[1][:, P * j:P * j + P], kvw[:, m % 2, j, 0:D], hotT[:, 2 * j:2 * j + 2, 0, :],
                                     start=True, stop=True)
                last.then_inc(s.k_psum, 1)

            def values(g, m):
                wait(pe, s.v_stored, g)
                for b in range(SG):
                    last = pe.matmul(ps[6 + b // 4][:, D * (b % 4):D * (b % 4) + D], hotT[:, b], kvw[:, m % 2, b // 2, D:2 * D],
                                     start=True, stop=True)
                last.then_inc(s.v_psum, 1)

            def queries(g, m):
                pe.wait_ge(s.hT_ready, g + 1)
                wait(pe, s.k_stored, g - 2)
                wait(pe, s.q_stored, g)
                pe.matmul(ps[1], wq[:, :], hT[:, m % 2, :], start=True, stop=True).then_inc(s.q_psum, 1)

            def score(g, m):
                pe.wait_ge(s.q_stored, g + 1)
                pe.wait_ge(s.ctx_loaded, 16 * (g + 1))
                wait(pe, s.hot_ready, g)
                pe.matmul(ps[2], k.identb[:, :], k.same2b[:, :], start=True, stop=False, skip_group_check=True)
                for j in range(TG):
                    last = pe.matmul(ps[2][:, P * j:P * j + P], q[:, m % 2, P * j:P * j + P], ctxT[:, m, P * j:P * j + P],
                                     start=False, stop=True, skip_group_check=True)
                last.then_inc(s.score_psum, 1)

            def project(g, m):
                wait(pe, s.kvw_ready, g)
                for j in range(TG):
                    last = pe.matmul(ps[4 + j // 2][:, 2 * D * (j % 2):2 * D * (j % 2) + 2 * D], ctxT[:, m, P * j:P * j + P], wkv[:, :],
                                     start=True, stop=True)
                last.then_inc(s.kvw_psum, 1)

            def turn_hot(g, m):
                pe.wait_ge(s.hot_ready, g + 1)
                wait(pe, s.hotT_ready, g)
                four_transposes(pe, k, ps[3], hot).then_inc(s.hotT_psum, 1)

            pipeline(pe, k.NG, [(0, turn), (4, keys), (4, values), (1, queries), (3, project), (2, score), (3, turn_hot)], unroll=4)

        @block.scalar
        def _(act):
            finish_stats_act(act, k, s)

            def copy_hT(g, m):
                act.wait_ge(s.hT_psum, g + 1)
                wait(act, s.q_psum, g - 1)
                act.copy(hT[:, m % 2, :], ps[0]).then_inc(s.hT_ready, 1)

            def store_k(g, m):
                act.wait_ge(s.k_psum, g + 1)
                settle(act, k)
                act.copy(r.kT[:, bass.ds(GT * g, GT)], ps[1]).then_inc(s.k_stored, 1)

            def store_q(g, m):
                act.wait_ge(s.q_psum, g + 1)
                wait(act, s.score_psum, g - 1)
                settle(act, k)
                act.copy(q[:, m % 2, :], ps[1])
                act.copy(r.qT[:, bass.ds(GT * g, GT)], ps[1]).then_inc(s.q_stored, 1)

            def copy_hotT(g, m):
                act.wait_ge(s.hotT_psum, g + 1)
                wait(act, s.v_psum, g)
                for copy in range(2):
                    last = act.copy(hotT[:, :, copy, :], ps[3].rearrange("p (b n) -> p b n", n=S))
                last.then_inc(s.hotT_ready, 1)

            pipeline(act, k.NG, [(0, copy_hT), (4, store_k), (1, store_q), (3, copy_hotT)], unroll=4)

        @block.vector
        def _(dve):
            finish_stats_dve(dve, k, s)

            def norm(g, m):
                wait(dve, s.hT_psum, g)
                layernorm(dve, k, h, g).then_inc(s.h_ready, 1)

            def store_v(g, m):
                dve.wait_ge(s.v_psum, g + 1)
                store_v2(dve, k, r, g).then_inc(s.v_stored, 1)

            def copy_kvw(g, m):
                dve.wait_ge(s.kvw_psum, g + 1)
                wait(dve, s.v_psum, g - 1)
                dve.tensor_copy(kvw[:, m % 2].rearrange("p t n -> p (t n)"), k.banks[:, 4:6, :].rearrange("p b n -> p (b n)"))\
                    .then_inc(s.kvw_ready, 1)

            def choose(g, m):
                chain = Chain(dve, s.hot_chain, g, 5)
                dve.wait_ge(s.score_psum, g + 1)
                wait(dve, s.hotT_psum, g)
                first_max(dve, chain, ps[2].rearrange("p (t n) -> p t n", n=P), k.count128,
                          OneHot(top=top[:, 0, :], index=top[:, 1, :], hot=hot[:, :, :]))
                dve.sem_inc(s.hot_ready, 1)
                chain.close()

            pipeline(dve, k.NG, [(0, norm), (4, store_v), (3, copy_kvw), (2, choose)], unroll=4)


def phase_l2_attention(nc, k):
    with ExitStack() as ctx:
        r = residents(nc, k, ctx, "l2")
        l2_projections(nc, k, r)
        attention_core(nc, k, "l2a", r, float(HD) ** -0.5, "L2_xattn_WcT")



HALF = HD // 2
LOOKBACK = 4
TWO_PI_HIGH = 6.28125
TWO_PI_LOW = 2 * np.pi - 6.28125


def l3_projections(nc, k, r):
    NP = k.NT + 1
    with ExitStack() as ctx:
        def sb(name, shape, dt=F32):
            return ctx.enter_context(nc.sbuf_tensor(f"l3p_{name}", shape, dt))

        s = sems(nc, ctx, "l3p", "var_ready std_ready rstd_ready weights t_chain angles_ready trig_ready table_ready ctx_loaded "
                 "h_ready hT_psum hT_ready q_psum q_chain q_roped qT_psum q_stored k_psum k_chain k_roped kT_psum k_stored v_psum v_stored")
        wq = sb("wq", [P, 2 * D])
        wk = sb("wk", [P, 2 * D])
        wv = sb("wv", [P, D])
        posi = sb("posi", [P, NP], I32)
        segi = sb("segi", [P, k.NT], I32)
        pos = sb("pos", [P, NP])
        angle = sb("angle", [P, 2, NP, HALF])
        turns = sb("turns", [P, 2, NP, HALF])
        table = sb("table", [P, 2, NP, HD])
        ctxT = sb("ctxT", [P, 2, GT])
        ctx2 = sb("ctx2", [P, 2, SG, 2, S])
        h = sb("h", [P, TG, D])
        hT = sb("hT", [P, 2, GT])
        part = sb("part", [P, TG, D])
        qr = sb("qr", [P, TG, D])
        kr = sb("kr", [P, TG, D])
        ps = k.psum
        block = ctx.enter_context(nc.Block())

        @block.sync
        def _(sp):
            for dst, name in ((wq, "L3_xattn_Wq2"), (wk, "L3_xattn_Wk2"), (wv, "L3_xattn_Wv"), (posi, "positions"), (segi, "segments")):
                sp.dma_start(dst[:, :], k.dram[name]).then_inc(s.weights, 16)

            def load(g, m):
                wait(sp, s.v_psum, g - 1)
                wait(sp, s.ctx_loaded, 48 * g)
                group = k.dram["ctxT"][:, bass.ds(g * GT, GT)]
                sp.dma_start(ctxT[:, m, :], group).then_inc(s.ctx_loaded, 16)
                for copy in range(2):
                    sp.dma_start(ctx2[:, m, :, copy, :], group.rearrange("c (q n) -> c q n", n=S)).then_inc(s.ctx_loaded, 16)

            pipeline(sp, k.NG, [(0, load)])

        @block.tensor
        def _(pe):
            pe.wait_ge(s.weights, 16 * 5)

            def turn(g, m):
                pe.wait_ge(s.h_ready, g + 1)
                wait(pe, s.hT_ready, g)
                wait(pe, s.q_stored, g - 2)
                four_transposes(pe, k, ps[0], h).then_inc(s.hT_psum, 1)

            def both(bank, lhsT, w):
                for j in range(TG):
                    last = pe.matmul(ps[bank + j // 2][:, 2 * D * (j % 2):2 * D * (j % 2) + 2 * D], lhsT[:, P * j:P * j + P], w[:, :],
                                     start=True, stop=True)
                return last

            def project(g, m):
                pe.wait_ge(s.ctx_loaded, 48 * (g + 1))
                wait(pe, s.k_roped, g)
                both(4, ctxT[:, m], wk).then_inc(s.k_psum, 1)
                pe.wait_ge(s.hT_ready, g + 1)
                wait(pe, s.q_roped, g)
                both(2, hT[:, m], wq).then_inc(s.q_psum, 1)
                wait(pe, s.v_stored, g)
                for q in range(SG):
                    last = pe.matmul(ps[6 + q // 4][:, D * (q % 4):D * (q % 4) + D], ctx2[:, m, q], wv[:, :], start=True, stop=True)
                last.then_inc(s.v_psum, 1)

            def turn_k(g, m):
                pe.wait_ge(s.k_roped, g + 1)
                wait(pe, s.k_stored, g)
                four_transposes(pe, k, ps[1], kr).then_inc(s.kT_psum, 1)

            def turn_q(g, m):
                pe.wait_ge(s.q_roped, g + 1)
                pe.wait_ge(s.hT_ready, upto(g + 3, k.NG))
                wait(pe, s.q_stored, g)
                four_transposes(pe, k, ps[0], qr).then_inc(s.qT_psum, 1)

            pipeline(pe, k.NG, [(0, turn), (2, turn_k), (2, turn_q), (1, project)])

        @block.scalar
        def _(act):
            finish_stats_act(act, k, s)
            act.wait_ge(s.angles_ready, 1)
            act.activation(angle[:, :, :, :].rearrange("p a b c -> p (a b c)"), angle[:, :, :, :].rearrange("p a b c -> p (a b c)"),
                           ACT.Sin).then_inc(s.trig_ready, 1)

            def copy_hT(g, m):
                act.wait_ge(s.hT_psum, g + 1)
                wait(act, s.q_psum, g - 1)
                act.copy(hT[:, m, :], ps[0]).then_inc(s.hT_ready, 1)

            def store_k(g, m):
                act.wait_ge(s.kT_psum, g + 1)
                settle(act, k)
                act.copy(r.kT[:, bass.ds(GT * g, GT)], ps[1]).then_inc(s.k_stored, 1)

            def store_q(g, m):
                act.wait_ge(s.qT_psum, g + 1)
                settle(act, k)
                act.copy(r.qT[:, bass.ds(GT * g, GT)], ps[0]).then_inc(s.q_stored, 1)

            pipeline(act, k.NG, [(0, copy_hT), (2, store_k), (2, store_q)])

        @block.vector
        def _(dve):
            finish_stats_dve(dve, k, s)
            dve.wait_ge(s.weights, 16 * 5)
            chain = Chain(dve, s.t_chain)
            go = lambda ins: chain.wait(chain.did(ins))
            flat = lambda ap: ap.rearrange("p a b -> p (a b)")
            cos, sin = angle[:, 0], angle[:, 1]
            chain.did(dve.tensor_copy(r.segments[:, :], segi[:, :]))
            go(dve.tensor_copy(pos[:, :], posi[:, :]))
            go(dve.tensor_scalar(pos[:, :], pos[:, :], 0.0, 1023.0, ALU.max, ALU.min))
            go(dve.tensor_tensor(sin, pos[:, :].unsqueeze(2).to_broadcast([P, NP, HALF]), k.frequency.unsqueeze(1).to_broadcast([P, NP, HALF]), ALU.mult))
            go(dve.tensor_scalar(turns[:, 0], sin, 1 / (2 * np.pi), ROUND, ALU.mult, ALU.add))
            go(dve.tensor_scalar(turns[:, 0], turns[:, 0], ROUND, None, ALU.subtract))
            go(dve.scalar_tensor_tensor(out=sin, in0=turns[:, 0], scalar=-TWO_PI_HIGH, in1=sin, op0=ALU.mult, op1=ALU.add))
            go(dve.scalar_tensor_tensor(out=sin, in0=turns[:, 0], scalar=-TWO_PI_LOW, in1=sin, op0=ALU.mult, op1=ALU.add))
            go(dve.tensor_scalar(cos, sin, np.pi / 2, None, ALU.add))
            go(dve.tensor_scalar(turns[:, 1], cos, np.pi, -2 * np.pi, ALU.is_gt, ALU.mult))
            go(dve.tensor_tensor(cos, cos, turns[:, 1], ALU.add))
            dve.tensor_scalar(angle[:, :, :, :].rearrange("p a b c -> p (a b c)"), angle[:, :, :, :].rearrange("p a b c -> p (a b c)"),
                              3.1415925, -3.1415925, ALU.min, ALU.max).then_inc(s.angles_ready, 1)
            dve.wait_ge(s.trig_ready, 1)
            for half in range(2):
                dims = slice(HALF * half, HALF * half + HALF)
                chain.did(dve.tensor_copy(table[:, 0, :, dims], cos))
                chain.did(dve.tensor_scalar(table[:, 1, :, dims], sin, 2.0 * half - 1.0, None, ALU.mult))
            chain.wait()

            def norm(g, m):
                wait(dve, s.hT_psum, g)
                layernorm(dve, k, h, g).then_inc(s.h_ready, 1)

            def rope(out, bank, cos, sin, chain, done):
                for b in range(2):
                    tiles = slice(2 * b, 2 * b + 2)
                    src = ps[bank + b].rearrange("p (t a h e) -> p t a h e", t=2, a=2, e=HD)
                    for a, (trig, dst) in enumerate(((cos, out), (sin, part))):
                        for t in range(2):
                            chain.did(dve.tensor_tensor(dst[:, 2 * b + t].rearrange("p (h e) -> p h e", e=HD), src[:, t, a],
                                                        trig(2 * b + t), ALU.mult))
                chain.wait()
                dve.tensor_tensor(out[:, :, :], out[:, :, :], part[:, :, :], ALU.add).then_inc(done, 1)

            def rope_k(g, m):
                dve.wait_ge(s.k_psum, g + 1)
                wait(dve, s.kT_psum, g)
                wait(dve, s.q_roped, g)
                chain = Chain(dve, s.k_chain, g, 8)
                rope(kr, 4, *(lambda j, a=a: table[:, a, k.NT, :].unsqueeze(1).to_broadcast([P, H, HD]) for a in range(2)),
                     chain, s.k_roped)
                chain.close()

            def rope_q(g, m):
                dve.wait_ge(s.q_psum, g + 1)
                wait(dve, s.qT_psum, g)
                dve.wait_ge(s.k_roped, g + 1)
                chain = Chain(dve, s.q_chain, g, 8)
                rope(qr, 2, *(lambda j, a=a: table[:, a, bass.ds(TG * g + j, 1), :].to_broadcast([P, H, HD]) for a in range(2)),
                     chain, s.q_roped)
                chain.close()

            def store_v(g, m):
                dve.wait_ge(s.v_psum, g + 1)
                store_v2(dve, k, r, g).then_inc(s.v_stored, 1)

            pipeline(dve, k.NG, [(0, norm), (1, rope_k), (1, rope_q), (1, store_v)])


def l3_masks(nc, k, r, masks):
    with ExitStack() as ctx:
        s = sems(nc, ctx, "l3m", "chain")
        away = ctx.enter_context(nc.sbuf_tensor("l3m_away", [P, k.NT, S], F32))
        far = ctx.enter_context(nc.sbuf_tensor("l3m_far", [P, k.NT, S], F32))
        block = ctx.enter_context(nc.Block())

        @block.vector
        def _(dve):
            chain = Chain(dve, s.chain)
            chain.wait(chain.did(dve.tensor_tensor(away[:, :, :], k.count64.unsqueeze(1).to_broadcast([P, k.NT, S]),
                                                   r.segments[:, :].unsqueeze(2).to_broadcast([P, k.NT, S]), ALU.subtract)))
            chain.wait(chain.did(dve.tensor_scalar(far[:, :, :], away[:, :, :], float(-LOOKBACK), NEG, ALU.is_lt, ALU.mult)))
            chain.wait(chain.did(dve.tensor_scalar(away[:, :, :], away[:, :, :], 0.0, NEG, ALU.is_gt, ALU.mult)))
            chain.wait(chain.did(dve.tensor_tensor(masks[:, :, :], away[:, :, :], far[:, :, :], ALU.add)))


def phase_l3_attention(nc, k):
    with ExitStack() as ctx:
        r = residents(nc, k, ctx, "l3", segments=True)
        l3_projections(nc, k, r)
        masks = ctx.enter_context(nc.sbuf_tensor("l3_masks", [P, k.NT, S], BF16))
        mask_b = ctx.enter_context(nc.sbuf_tensor("l3_mask", [P, 2, S], BF16))
        l3_masks(nc, k, r, masks)
        ready = ctx.enter_context(nc.semaphore("l3_mask_ready"))

        def copy(pool, t, par, used):
            wait(pool, used, 2 * (t - 1))
            settle(pool, k)
            pool.tensor_copy(mask_b[:, par], masks[:, bass.ds(t, 1), :]).then_inc(ready, 1)

        def rhs(pe, t, par):
            pe.wait_ge(ready, t + 1)
            return mask_b[:, par].unsqueeze(1).to_broadcast([P, 4, S])

        attention_core(nc, k, "l3a", r, float(HD) ** -0.5, "L3_xattn_Wo", Mask(rhs=rhs, copy=copy))



W_MOST = 127.0
A_MOST = 32767.0


def phase_l3_ffn(nc, k):
    FC = F0 // P
    with ExitStack() as ctx:
        def sb(name, shape, dt=F32):
            return ctx.enter_context(nc.sbuf_tensor(f"l3f_{name}", shape, dt))

        w = namedtuple("L3Ffn", "in_T win wout scale b_in b_out most inv hidden")(
            in_T=sb("in_T", [P, FC, D]), win=sb("win", [P, FC, P], BF16), wout=sb("wout", [P, FC, D]),
            scale=sb("scale", [P, 4, FC]), b_in=sb("b_in", [P, FC]), b_out=sb("b_out", [P, D]),
            most=sb("most", [P, 4]), inv=sb("inv", [P, 4]), hidden=sb("hidden", [P, FC, k.NT * P]))
        l3_ffn_scales(nc, k, w)
        l3_ffn_up(nc, k, w)
        l3_ffn_down(nc, k, w)


def most_of_all(pool, s, w, n):
    pool.wait_ge(s.most_ready, 1)
    pool.partition_all_reduce(w.inv[:, n:n + 1], w.most[:, n:n + 1], P, bass.bass_isa.ReduceOp.max).then_inc(s.all_ready, 1)


def activation_scale(dve, chain, w, n):
    chain.wait(chain.did(dve.tensor_scalar(w.inv[:, n:n + 1], w.inv[:, n:n + 1], 1e-8, None, ALU.max)))
    chain.wait(chain.did(dve.reciprocal(w.most[:, n:n + 1], w.inv[:, n:n + 1])))
    chain.did(dve.tensor_scalar(w.most[:, n:n + 1], w.most[:, n:n + 1], A_MOST, None, ALU.mult))
    chain.wait(chain.did(dve.tensor_scalar(w.inv[:, n:n + 1], w.inv[:, n:n + 1], 1.0 / A_MOST, None, ALU.mult)))


def l3_ffn_scales(nc, k, w):
    FC = F0 // P
    with ExitStack() as ctx:
        s = sems(nc, ctx, "l3s", "var_ready std_ready rstd_ready weights w_chain win_ready win_psum h_chain most_ready all_ready")
        h = ctx.enter_context(nc.sbuf_tensor("l3s_h", [P, 2, TG, D], F32))
        top = ctx.enter_context(nc.sbuf_tensor("l3s_top", [P, 2], F32))
        block = ctx.enter_context(nc.Block())

        @block.sync
        def _(sp):
            for dst, name in ((w.in_T, "L3_ffn_W_inT"), (w.wout, "L3_ffn_W_out")):
                sp.dma_start(dst[:, :, :].rearrange("p a b -> p (a b)"), k.dram[name]).then_inc(s.weights, 16)
            for dst, name in ((w.b_in, "L3_ffn_b_in"), (w.b_out, "L3_ffn_b_out")):
                sp.dma_start(dst[:, :], k.dram[name]).then_inc(s.weights, 16)

        @block.tensor
        def _(pe):
            pe.wait_ge(s.win_ready, 1)
            for c in range(FC):
                last = pe.transpose(k.psum[0][:, P * c:P * c + P], w.in_T[:, c, :], k.ident)
            last.then_inc(s.win_psum, 1)

        @block.scalar
        def _(act):
            finish_stats_act(act, k, s)
            act.wait_ge(s.win_psum, 1)
            act.copy(w.win[:, :, :].rearrange("p a b -> p (a b)"), k.psum[0])

        @block.gpsimd
        def _(pool):
            most_of_all(pool, s, w, 0)

        @block.vector
        def _(dve):
            finish_stats_dve(dve, k, s)
            chain = Chain(dve, s.w_chain)
            go = lambda ins: chain.wait(chain.did(ins))
            dve.wait_ge(s.weights, 16 * 4)
            go(dve.memset(w.most[:, :], 0.0))
            for n, m in enumerate((w.in_T, w.wout)):
                whole = m[:, :, :]
                wide = lambda ap: ap.unsqueeze(2).to_broadcast([P, FC, D])
                amax, scale = w.scale[:, 2 * n, :], w.scale[:, 2 * n + 1, :]
                go(dve.tensor_reduce(amax, whole, AX_X, ALU.max, apply_absolute_value=True))
                go(dve.tensor_scalar(amax, amax, 1e-8, None, ALU.max))
                go(dve.reciprocal(scale, amax))
                chain.did(dve.tensor_scalar(scale, scale, W_MOST, None, ALU.mult))
                go(dve.tensor_scalar(amax, amax, 1.0 / W_MOST, None, ALU.mult))
                go(dve.tensor_tensor(whole, whole, wide(scale), ALU.mult))
                go(dve.tensor_scalar(whole, whole, ROUND, ROUND, ALU.add, ALU.subtract))
                if n == 0:
                    dve.tensor_scalar(whole, whole, W_MOST, -W_MOST - 1, ALU.min, ALU.max).then_inc(s.win_ready, 1)
                else:
                    go(dve.tensor_scalar(whole, whole, W_MOST, -W_MOST - 1, ALU.min, ALU.max))
                    go(dve.tensor_tensor(whole, whole, wide(amax), ALU.mult))

            def largest(g, m):
                chain = Chain(dve, s.h_chain, g, 3)
                wait(dve, s.h_chain, 3 * (g - 1))
                chain.did(layernorm(dve, k, h[:, m], g))
                chain.wait()
                chain.wait(chain.did(dve.tensor_reduce(top[:, m:m + 1], h[:, m].rearrange("p t c -> p (t c)"), AX_X, ALU.max,
                                                       apply_absolute_value=True)))
                chain.did(dve.tensor_tensor(w.most[:, 0:1], w.most[:, 0:1], top[:, m:m + 1], ALU.max))
                chain.wait()
                chain.close()

            pipeline(dve, k.NG, [(0, largest)])
            dve.sem_inc(s.most_ready, 1)


def l3_ffn_up(nc, k, w):
    FC = F0 // P
    with ExitStack() as ctx:
        def sb(name, shape, dt=F32):
            return ctx.enter_context(nc.sbuf_tensor(f"l3u_{name}", shape, dt))

        s = sems(nc, ctx, "l3u", "scale_chain scale_ready h_chain h_ready hT_psum high_ready split_ready f_psum f_ready f_chain most_ready all_ready")
        h = sb("h", [P, 2, TG, D])
        high = sb("high", [P, 2, GT], BF16)
        low = sb("low", [P, 2, GT], BF16)
        top = sb("top", [P, 2])
        ps = k.psum
        block = ctx.enter_context(nc.Block())

        @block.tensor
        def _(pe):
            def turn(g, m):
                pe.wait_ge(s.h_ready, g + 1)
                wait(pe, s.split_ready, g - 1)
                four_transposes(pe, k, ps[m], h[:, m]).then_inc(s.hT_psum, 1)

            def up(g, m):
                pe.wait_ge(s.split_ready, g + 1)
                wait(pe, s.f_ready, g)
                for c in range(FC):
                    pe.matmul(ps[4 + c], w.win[:, c, :], high[:, m, :], start=True, stop=False)
                    last = pe.matmul(ps[4 + c], w.win[:, c, :], low[:, m, :], start=False, stop=True)
                last.then_inc(s.f_psum, 1)

            pipeline(pe, k.NG, [(0, turn), (1, up)])

        @block.scalar
        def _(act):
            act.wait_ge(s.scale_ready, 1)

            def split(g, m):
                act.wait_ge(s.hT_psum, g + 1)
                wait(act, s.f_psum, g - 1)
                act.copy(high[:, m, :], ps[m]).then_inc(s.high_ready, 1)

            def gelu(g, m):
                act.wait_ge(s.f_psum, g + 1)
                settle(act, k)
                for c in range(FC):
                    last = act.activation(w.hidden[:, c, bass.ds(GT * g, GT)], ps[4 + c], ACT.Gelu,
                                          bias=w.b_in[:, c:c + 1], scale=w.scale[:, 0, c:c + 1])
                last.then_inc(s.f_ready, 1)

            pipeline(act, k.NG, [(0, split), (1, gelu)])

        @block.gpsimd
        def _(pool):
            most_of_all(pool, s, w, 1)

        @block.vector
        def _(dve):
            chain = Chain(dve, s.scale_chain)
            activation_scale(dve, chain, w, 0)
            dve.tensor_scalar(w.scale[:, 0, :], w.scale[:, 0, :], w.inv[:, 0:1], None, ALU.mult).then_inc(s.scale_ready, 1)

            def quantise(g, m):
                chain = Chain(dve, s.h_chain, g, 3)
                wait(dve, s.hT_psum, g - 1)
                chain.did(layernorm(dve, k, h[:, m], g))
                chain.wait()
                chain.wait(chain.did(dve.tensor_scalar(h[:, m], h[:, m], w.most[:, 0:1], None, ALU.mult)))
                chain.wait(chain.did(dve.tensor_scalar(h[:, m], h[:, m], ROUND, ROUND, ALU.add, ALU.subtract)))
                dve.tensor_scalar(h[:, m], h[:, m], A_MOST, -A_MOST - 1, ALU.min, ALU.max).then_inc(s.h_ready, 1)
                chain.close()

            def lower(g, m):
                dve.wait_ge(s.high_ready, g + 1)
                dve.tensor_tensor(low[:, m, :], ps[m], high[:, m, :], ALU.subtract).then_inc(s.split_ready, 1)

            def largest(g, m):
                dve.wait_ge(s.f_ready, g + 1)
                wait(dve, s.f_chain, 2 * (g - 1))
                dve.tensor_copy(k.pad2[:, :], k.pad[:, :])
                dve.tensor_reduce(top[:, m:m + 1], w.hidden[:, :, bass.ds(GT * g, GT)], mybir.AxisListType.XY, ALU.max,
                                  apply_absolute_value=True).then_inc(s.f_chain, 1)
                dve.wait_ge(s.f_chain, 2 * g + 1)
                dve.tensor_tensor(w.most[:, 1:2], w.most[:, 1:2], top[:, m:m + 1], ALU.max).then_inc(s.f_chain, 1)
                dve.wait_ge(s.f_chain, 2 * g + 2)

            pipeline(dve, k.NG, [(0, quantise), (0, lower), (2, largest)])
            dve.sem_inc(s.most_ready, 1)


def l3_ffn_down(nc, k, w):
    FC = F0 // P
    with ExitStack() as ctx:
        def sb(name, shape, dt=F32):
            return ctx.enter_context(nc.sbuf_tensor(f"l3d_{name}", shape, dt))

        s = sems(nc, ctx, "l3d", "scale_chain f_chain f_ready y_psum xb_ready xn_ready stored")
        f = sb("f", [P, 2, FC, GT])
        ps = k.psum
        out = k.dram["out"].rearrange("(t p) c -> p t c", p=P)
        block = ctx.enter_context(nc.Block())

        @block.gpsimd
        def _(pool):
            def store(g, m):
                pool.wait_ge(s.xn_ready, g + 1)
                wait(pool, s.stored, 16 * g)
                settle(pool, k)
                pool.dma_start(out[:, bass.ds(TG * g, TG), :], k.xn[:, m]).then_inc(s.stored, 16)

            pipeline(pool, k.NG, [(1, lambda g, m: xb_pool(pool, k, s, g, m, w.b_out)), (2, store)])
            pool.wait_ge(s.stored, 16 * k.NG)

        @block.tensor
        def _(pe):
            def down(g, m):
                pe.wait_ge(s.f_ready, g + 1)
                wait(pe, s.xn_ready, g - 1)
                for j in range(TG):
                    for c in range(FC):
                        last = pe.matmul(ps[m][:, D * j:D * j + D], f[:, m, c, P * j:P * j + P], w.wout[:, c, :],
                                         start=(c == 0), stop=(c == FC - 1))
                last.then_inc(s.y_psum, 1)

            pipeline(pe, k.NG, [(0, down)])

        @block.vector
        def _(dve):
            chain = Chain(dve, s.scale_chain)
            activation_scale(dve, chain, w, 1)

            def quantise(g, m):
                chain = Chain(dve, s.f_chain, g, 2)
                wait(dve, s.y_psum, g - 1)
                chain.wait(chain.did(dve.tensor_scalar(f[:, m], w.hidden[:, :, bass.ds(GT * g, GT)], w.most[:, 1:2], ROUND, ALU.mult, ALU.add)))
                chain.wait(chain.did(dve.tensor_scalar(f[:, m], f[:, m], ROUND, A_MOST, ALU.subtract, ALU.min)))
                dve.tensor_scalar(f[:, m], f[:, m], -A_MOST - 1, None, ALU.max).then_inc(s.f_ready, 1)
                chain.close()

            def new_x(g, m):
                dve.wait_ge(s.y_psum, g + 1)
                dve.wait_ge(s.xb_ready, g + 1)
                wait(dve, s.stored, 16 * (g - 1))
                dve.scalar_tensor_tensor(out=k.xn[:, m], in0=ps[m].rearrange("p (t c) -> p t c", c=D), scalar=w.inv[:, 1:2],
                                         in1=k.xb[:, m], op0=ALU.mult, op1=ALU.add).then_inc(s.xn_ready, 1)

            pipeline(dve, k.NG, [(0, quantise), (1, new_x)])



EXPERTS = 8


def phase_l2_ffn(nc, k):
    FC = F0 // P
    with ExitStack() as ctx:
        def sb(name, shape, dt=F32):
            return ctx.enter_context(nc.sbuf_tensor(f"l2f_{name}", shape, dt))

        cap = max(4, -(-k.NT * P // EXPERTS))
        w = namedtuple("L2Ffn", "cap slots rows hot gate coef slot back nw nb sent answers")(
            cap=cap, slots=EXPERTS * cap,
            rows=sb("rows", [P, k.NT, D]),
            hot=sb("hot", [P, k.NT, EXPERTS], BF16), gate=sb("gate", [P, k.NT]), coef=sb("coef", [P, k.NT, 2]),
            slot=sb("slot", [P, k.NT], I32), back=sb("back", [P, k.NT], I32),
            nw=sb("nw", [P, 1]), nb=sb("nb", [P, 1]),
            sent=nc.dram_tensor("l2f_sent", (EXPERTS * cap + k.NT * P, D), F32, kind="Internal").ap(),
            answers=nc.dram_tensor("l2f_answers", (EXPERTS * cap, D), F32, kind="Internal").ap())
        l2_ffn_gate(nc, k, w)
        l2_ffn_send(nc, k, w)
        l2_ffn_experts(nc, k, w)
        l2_ffn_gather(nc, k, w)


def l2_ffn_gate(nc, k, w):
    FC = F0 // P
    N = EXPERTS + 2
    with ExitStack() as ctx:
        def sb(name, shape, dt=F32):
            return ctx.enter_context(nc.sbuf_tensor(f"l2g_{name}", shape, dt))

        s = sems(nc, ctx, "l2g", X_SEMS + "weights zeroed zero_stored norm_chain norm_var norm_std norm_ready h_chain h_ready sum_ready copied aT_psum "
                 "aT_ready logit_psum g_chain shift_ready gate_exp gate_ready gate_copied f_psum f_ready y_psum y_chain")
        wg = sb("wg", [P, N])
        w1 = sb("w1", [P, FC, P])
        b1 = sb("b1", [P, FC])
        w2 = sb("w2", [P, FC, D])
        b2 = sb("b2", [P, D])
        zero = sb("zero", [P, 2048])
        both = sb("both", [P, k.NT])
        h = sb("h", [P, 2, TG, D])
        h1 = sb("h1", [P, 2, TG, D])
        aT = sb("aT", [P, 2, GT])
        gates = sb("gates", [P, 2, TG, N])
        work = sb("work", [P, 4, TG])
        hot = sb("hot", [P, 2, TG, EXPERTS])
        out4 = sb("out4", [P, 2, TG, 3])
        f = sb("f", [P, FC, GT])
        y = sb("y", [P, TG, D])
        ps = k.psum
        block = ctx.enter_context(nc.Block())

        @block.sync
        def _(sp):
            for dst, name in ((wg, "L2_ffn_wg_coef"), (b1, "L2_ffn_res_inter_b"), (b2, "L2_ffn_res_output_b"),
                              (w.nw, "L2_ffn_attn_nw"), (w.nb, "L2_ffn_attn_nb")):
                sp.dma_start(dst[:, :], k.dram[name]).then_inc(s.weights, 16)
            for dst, name in ((w1, "L2_ffn_res_inter_w"), (w2, "L2_ffn_res_output_w")):
                sp.dma_start(dst[:, :, :].rearrange("p a b -> p (a b)"), k.dram[name]).then_inc(s.weights, 16)
            sp.wait_ge(s.zeroed, 1)
            n = w.slots // P * D
            sent = w.sent[0:w.slots, :].rearrange("(p r) c -> p (r c)", p=P)
            for at in range(0, n, 2048):
                sp.dma_start(sent[:, at:at + 2048], zero[:, :]).then_inc(s.zero_stored, 16)
            sp.wait_ge(s.zero_stored, 16 * (n // 2048))

        @block.gpsimd
        def _(pool):
            def keep_rows(g, m):
                pool.wait_ge(s.h_ready, g + 1)
                settle(pool, k)
                pool.tensor_copy(w.rows[:, bass.ds(TG * g, TG), :], h[:, m])
                wait(pool, s.xn_ready, g - 1)
                settle(pool, k)
                pool.tensor_tensor(k.xb[:, m], k.x[:, bass.ds(TG * g, TG), :], h1[:, m], ALU.add).then_inc(s.xb_ready, 1)

            def keep_gates(g, m):
                pool.wait_ge(s.gate_ready, g + 1)
                settle(pool, k)
                pool.tensor_copy(w.hot[:, bass.ds(TG * g, TG), :], hot[:, m])
                pool.tensor_copy(w.gate[:, bass.ds(TG * g, TG)], out4[:, m, :, 0])
                pool.tensor_copy(w.coef[:, bass.ds(TG * g, TG), :], out4[:, m, :, 1:3]).then_inc(s.gate_copied, 1)

            pipeline(pool, k.NG, [(0, keep_rows), (1, keep_gates), (2, lambda g, m: x_copy_pool(pool, k, s, g, m))])

        @block.tensor
        def _(pe):
            pe.wait_ge(s.weights, 16 * 7)

            def turn(g, m):
                pe.wait_ge(s.h_ready, g + 1)
                wait(pe, s.aT_ready, g)
                four_transposes(pe, k, ps[0], h[:, m]).then_inc(s.aT_psum, 1)

            def up(g, m):
                pe.wait_ge(s.aT_ready, g + 1)
                wait(pe, s.shift_ready, g)
                for j in range(TG):
                    last = pe.matmul(ps[1][:, N * j:N * j + N], aT[:, m, P * j:P * j + P], wg[:, :], start=True, stop=True)
                last.then_inc(s.logit_psum, 1)
                wait(pe, s.f_ready, g)
                for c in range(FC):
                    last = pe.matmul(ps[4 + c], w1[:, c, :], aT[:, m, :], start=True, stop=True)
                last.then_inc(s.f_psum, 1)

            def down(g, m):
                pe.wait_ge(s.f_ready, g + 1)
                wait(pe, s.y_chain, 5 * (g - 1) + 1)
                for j in range(TG):
                    for c in range(FC):
                        last = pe.matmul(ps[2 + m][:, D * j:D * j + D], f[:, c, P * j:P * j + P], w2[:, c, :],
                                         start=(c == 0), stop=(c == FC - 1))
                last.then_inc(s.y_psum, 1)

            pipeline(pe, k.NG, [(0, turn), (2, down), (1, up)])

        @block.scalar
        def _(act):
            finish_stats_act(act, k, s)
            act.wait_ge(s.norm_var, 1)
            act.activation(both[:, :], both[:, :], ACT.Sqrt).then_inc(s.norm_std, 1)
            act.wait_ge(s.weights, 16 * 7)

            def scale(g, m):
                act.wait_ge(s.aT_psum, g + 1)
                wait(act, s.f_psum, g - 1)
                act.activation(aT[:, m, :], ps[0], ACT.Identity, bias=w.nb[:, 0:1], scale=w.nw[:, 0:1]).then_inc(s.aT_ready, 1)

            def exp(g, m):
                act.wait_ge(s.shift_ready, g + 1)
                act.activation(gates[:, m].rearrange("p a b -> p (a b)"), gates[:, m].rearrange("p a b -> p (a b)"), ACT.Exp)\
                    .then_inc(s.gate_exp, 1)

            def gelu(g, m):
                act.wait_ge(s.f_psum, g + 1)
                wait(act, s.y_psum, g)
                for c in range(FC):
                    last = act.activation(f[:, c, :], ps[4 + c], ACT.Gelu_apprx_tanh, bias=b1[:, c:c + 1])
                last.then_inc(s.f_ready, 1)

            pipeline(act, k.NG, [(0, scale), (1, exp), (1, gelu)])

        @block.vector
        def _(dve):
            dve.memset(zero[:, :], 0.0).then_inc(s.zeroed, 1)
            finish_stats_dve(dve, k, s)
            chain = Chain(dve, s.norm_chain)
            chain.wait(chain.did(dve.tensor_tensor(both[:, :], k.rstd[:, :], k.rstd[:, :], ALU.mult)))
            chain.wait(chain.did(dve.tensor_tensor(both[:, :], both[:, :], k.mv[:, :, 1], ALU.mult)))
            dve.tensor_scalar(both[:, :], both[:, :], 1e-12, None, ALU.add).then_inc(s.norm_var, 1)
            dve.wait_ge(s.norm_std, 1)
            chain.wait(chain.did(dve.reciprocal(both[:, :], both[:, :])))
            chain.wait(chain.did(dve.tensor_tensor(both[:, :], both[:, :], k.rstd[:, :], ALU.mult)))
            dve.wait_ge(s.weights, 16 * 7)

            def norm(g, m):
                wait(dve, s.xb_ready, g - 1)
                wait(dve, s.aT_psum, g - 1)
                layernorm(dve, k, h1[:, m], g)
                for j in range(TG):
                    t = TG * g + j
                    last = dve.tensor_scalar(h[:, m, j, :], k.x[:, bass.ds(t, 1), :], k.mv[:, bass.ds(t, 1), 0],
                                             both[:, bass.ds(t, 1)], ALU.subtract, ALU.mult)
                last.then_inc(s.h_ready, 1)

            def gate(g, m):
                chain = Chain(dve, s.g_chain, g, 13)
                go = lambda ins: chain.wait(chain.did(ins))
                G = gates[:, m]
                V = lambda n: work[:, n, :]
                wide = lambda ap, n: ap.unsqueeze(2).to_broadcast([P, TG, n])
                groups = ((slice(0, EXPERTS), 0, EXPERTS), (slice(EXPERTS, N), 1, 2))
                lg = ps[1][:, 0:TG * N].rearrange("p (t n) -> p t n", n=N)
                dve.wait_ge(s.logit_psum, g + 1)
                wait(dve, s.gate_ready, g)
                wait(dve, s.gate_copied, g - 1)
                for cols, n, size in groups:
                    chain.did(dve.tensor_reduce(V(n), lg[:, :, cols], AX_X, ALU.max))
                chain.wait()
                chain.did(dve.tensor_tensor(G[:, :, groups[0][0]], lg[:, :, groups[0][0]], wide(V(0), EXPERTS), ALU.subtract))
                chain.wait()
                dve.tensor_tensor(G[:, :, groups[1][0]], lg[:, :, groups[1][0]], wide(V(1), 2), ALU.subtract).then_inc(s.shift_ready, 1)
                dve.wait_ge(s.gate_exp, g + 1)
                for cols, n, size in groups:
                    chain.did(dve.tensor_reduce(V(n), G[:, :, cols], AX_X, ALU.add))
                chain.wait()
                go(dve.reciprocal(work[:, 0:2, :], work[:, 0:2, :]))
                chain.did(dve.tensor_tensor(out4[:, m, :, 1:3], G[:, :, groups[1][0]], wide(V(1), 2), ALU.mult))
                go(dve.tensor_tensor(G[:, :, groups[0][0]], G[:, :, groups[0][0]], wide(V(0), EXPERTS), ALU.mult))
                first_max(dve, chain, G[:, :, groups[0][0]], k.count8, OneHot(top=V(2), index=V(3), hot=hot[:, m]))
                dve.tensor_copy(out4[:, m, :, 0], V(2)).then_inc(s.gate_ready, 1)
                chain.close()

            def new_x(g, m):
                chain = Chain(dve, s.y_chain, g, 5)
                dve.wait_ge(s.y_psum, g + 1)
                wait(dve, s.xn_ready, g)
                chain.did(dve.tensor_tensor(y[:, :, :], ps[2 + m].rearrange("p (t c) -> p t c", c=D),
                                            b2[:, :].unsqueeze(1).to_broadcast([P, TG, D]), ALU.add))
                chain.wait()
                for j in range(TG):
                    chain.did(dve.tensor_scalar(y[:, j, :], y[:, j, :], out4[:, m, j, 1:2], None, ALU.mult))
                chain.wait()

                def add(xn):
                    dve.tensor_tensor(xn, y[:, :, :], k.xb[:, m], ALU.add).then_inc(s.xn_ready, 1)

                x_update_dve(dve, k, s, g, m, add)
                chain.close()

            pipeline(dve, k.NG, [(0, norm), (1, gate), (2, new_x)])


def l2_ffn_send(nc, k, w):
    NT = k.NT
    with ExitStack() as ctx:
        def sb(name, shape, dt=F32):
            return ctx.enter_context(nc.sbuf_tensor(f"l2s_{name}", shape, dt))

        s = sems(nc, ctx, "l2s", "chain count_psum slots_ready sent")
        place = sb("place", [P, NT, EXPERTS])
        run = sb("run", [P, 2, NT, EXPERTS])
        one = sb("one", [P, 8, NT])
        tri = sb("tri", [P, P], BF16)
        ones = sb("ones", [P, P], BF16)
        ps = k.psum
        block = ctx.enter_context(nc.Block())

        @block.tensor
        def _(pe):
            pe.wait_ge(s.chain, 2)
            hot = w.hot[:, :, :].rearrange("p t e -> p (t e)")
            pe.matmul(ps[0][:, 0:NT * EXPERTS], tri[:, :], hot, start=True, stop=True)
            pe.matmul(ps[1][:, 0:NT * EXPERTS], ones[:, :], hot, start=True, stop=True).then_inc(s.count_psum, 1)

        @block.vector
        def _(dve):
            chain = Chain(dve, s.chain)
            go = lambda ins: chain.wait(chain.did(ins))
            chain.did(dve.tensor_copy(tri[:, :], k.before))
            chain.did(dve.tensor_copy(ones[:, :], k.ones))
            dve.wait_ge(s.count_psum, 1)
            within = ps[0][:, 0:NT * EXPERTS].rearrange("p (t e) -> p t e", e=EXPERTS)
            totals = ps[1][:, 0:NT * EXPERTS].rearrange("p (t e) -> p t e", e=EXPERTS)
            chain.did(dve.memset(run[:, 0, 0:1, :], 0.0))
            go(dve.tensor_copy(run[:, 0, 1:NT, :], totals[:, 0:NT - 1, :]))
            side, step = 0, 1
            while step < NT:
                chain.did(dve.tensor_copy(run[:, 1 - side, 0:step, :], run[:, side, 0:step, :]))
                go(dve.tensor_tensor(run[:, 1 - side, step:NT, :], run[:, side, step:NT, :], run[:, side, 0:NT - step, :], ALU.add))
                side, step = 1 - side, 2 * step
            go(dve.tensor_tensor(place[:, :, :], within, run[:, side], ALU.add))
            go(dve.tensor_tensor(place[:, :, :], place[:, :, :], w.hot[:, :, :], ALU.mult))
            place1, first, keep, slot, spare, back = (one[:, n, :] for n in range(6))
            go(dve.tensor_reduce(place1, place[:, :, :], AX_X, ALU.add))
            go(dve.tensor_tensor(place[:, :, :], k.count8.unsqueeze(1).to_broadcast([P, NT, EXPERTS]), w.hot[:, :, :], ALU.mult))
            go(dve.tensor_reduce(first, place[:, :, :], AX_X, ALU.add))
            go(dve.tensor_scalar(first, first, float(EXPERTS), float(w.cap), ALU.add, ALU.mult))
            go(dve.tensor_tensor(slot, first, place1, ALU.add))
            chain.did(dve.tensor_scalar(keep, place1, float(w.cap), None, ALU.is_lt))
            go(dve.tensor_tensor(spare, slot, k.token[:, 0:NT], ALU.subtract))
            go(dve.tensor_scalar(spare, spare, float(w.slots), None, ALU.subtract))
            go(dve.tensor_tensor(spare, spare, keep, ALU.mult))
            go(dve.tensor_tensor(spare, spare, k.token[:, 0:NT], ALU.add))
            go(dve.tensor_scalar(w.slot[:, :], spare, float(w.slots), None, ALU.add))
            chain.did(dve.tensor_scalar(w.back[:, :], slot, float(w.slots - 1), None, ALU.min))
            go(dve.tensor_tensor(w.gate[:, :], w.gate[:, :], keep, ALU.mult))
            go(dve.tensor_tensor(w.gate[:, :], w.gate[:, :], w.coef[:, :, 1], ALU.mult))
            dve.sem_inc(s.slots_ready, 1)

        @block.gpsimd
        def _(pool):
            pool.wait_ge(s.slots_ready, 1)
            for t in range(NT):
                pool.indirect_dma_start(out=w.sent, out_offset=bass.IndirectOffsetOnAxis(ap=w.slot[:, t:t + 1], axis=0),
                                        in_=w.rows[:, t, :], in_offset=None).then_inc(s.sent, 16)
            pool.wait_ge(s.sent, 16 * NT)


def l2_ffn_experts(nc, k, w):
    FC = F0 // P
    C = min(GT, w.cap)
    CT = C // P
    per = w.cap // C
    with ExitStack() as ctx:
        def sb(name, shape, dt=F32):
            return ctx.enter_context(nc.sbuf_tensor(f"l2e_{name}", shape, dt))

        s = sems(nc, ctx, "l2e", "weights rows_loaded rT_psum rT_ready f_psum f_ready y_psum y_ready stored")
        set_cols = F0 + FC * D + FC + D
        sets = sb("sets", [P, 2, set_cols])
        w1 = sets[:, :, 0:F0]
        w2 = sets[:, :, F0:F0 + FC * D].rearrange("p s (c n) -> p s c n", n=D)
        b1 = sets[:, :, F0 + FC * D:F0 + FC * D + FC]
        b2 = sets[:, :, set_cols - D:]
        rows = sb("rows", [P, 2, CT, D])
        rT = sb("rT", [P, 2, C])
        f = sb("f", [P, FC, C])
        y = sb("y", [P, 2, CT, D])
        ps = k.psum
        items = EXPERTS * per
        block = ctx.enter_context(nc.Block())
        d = k.dram

        def expert(m):
            return (m // per) % 2

        @block.sync
        def _(sp):
            def load(n, m):
                wait(sp, s.rT_psum, n - 1)
                wait(sp, s.rows_loaded, 16 * n)
                sp.dma_start(rows[:, m % 2], w.sent[bass.ds(C * n, C), :].rearrange("(t p) c -> p t c", p=P)).then_inc(s.rows_loaded, 16)

            pipeline(sp, items, [(0, load)], unroll=2 * per)

        @block.tensor
        def _(pe):
            def turn(n, m):
                pe.wait_ge(s.rows_loaded, 16 * (n + 1))
                wait(pe, s.rT_ready, n)
                for j in range(CT):
                    last = pe.transpose(ps[0][:, P * j:P * j + P], rows[:, m % 2, j, :], k.ident)
                last.then_inc(s.rT_psum, 1)

            def up(n, m):
                pe.wait_ge(s.rT_ready, n + 1)
                pe.wait_ge(s.weights, (n - m % per) * (16 // per) + 16)
                wait(pe, s.f_ready, n)
                for c in range(FC):
                    last = pe.matmul(ps[4 + c][:, 0:C], w1[:, expert(m), P * c:P * c + P], rT[:, m % 2, :], start=True, stop=True)
                last.then_inc(s.f_psum, 1)

            def down(n, m):
                pe.wait_ge(s.f_ready, n + 1)
                wait(pe, s.y_ready, n - 1)
                for j in range(CT):
                    for c in range(FC):
                        last = pe.matmul(ps[2 + m % 2][:, D * j:D * j + D], f[:, c, P * j:P * j + P], w2[:, expert(m), c, :],
                                         start=(c == 0), stop=(c == FC - 1))
                last.then_inc(s.y_psum, 1)

            pipeline(pe, items, [(0, turn), (2, down), (1, up)], unroll=2 * per)

        @block.scalar
        def _(act):
            def scale(n, m):
                act.wait_ge(s.rT_psum, n + 1)
                wait(act, s.f_psum, n - 1)
                act.activation(rT[:, m % 2, :], ps[0][:, 0:C], ACT.Identity, bias=w.nb[:, 0:1], scale=w.nw[:, 0:1]).then_inc(s.rT_ready, 1)

            def gelu(n, m):
                act.wait_ge(s.f_psum, n + 1)
                wait(act, s.y_psum, n)
                for c in range(FC):
                    last = act.activation(f[:, c, :], ps[4 + c][:, 0:C], ACT.Gelu_apprx_tanh, bias=b1[:, expert(m), c:c + 1])
                last.then_inc(s.f_ready, 1)

            pipeline(act, items, [(0, scale), (1, gelu)], unroll=2 * per)

        @block.vector
        def _(dve):
            def bias(n, m):
                dve.wait_ge(s.y_psum, n + 1)
                wait(dve, s.stored, 16 * (n - 1))
                dve.tensor_tensor(y[:, m % 2], ps[2 + m % 2][:, 0:CT * D].rearrange("p (t c) -> p t c", c=D),
                                  b2[:, expert(m), :].unsqueeze(1).to_broadcast([P, CT, D]), ALU.add).then_inc(s.y_ready, 1)

            pipeline(dve, items, [(2, bias)], unroll=2 * per)

        @block.gpsimd
        def _(pool):
            def load_set(n, m):
                if m % per == 0:
                    wait(pool, s.y_ready, n - per)
                    wait(pool, s.weights, n * (16 // per))
                    settle(pool, k)
                    pool.dma_start(sets[:, expert(m), :], d["L2_ffn_expert_sets"][bass.ds(n * (P // per), P), :]).then_inc(s.weights, 16)

            def store(n, m):
                pool.wait_ge(s.y_ready, n + 1)
                wait(pool, s.stored, 16 * n)
                settle(pool, k)
                pool.dma_start(w.answers[bass.ds(C * n, C), :].rearrange("(t p) c -> p t c", p=P), y[:, m % 2]).then_inc(s.stored, 16)

            pipeline(pool, items, [(0, load_set), (2, store)], unroll=2 * per)
            pool.wait_ge(s.stored, 16 * items)


def l2_ffn_gather(nc, k, w):
    with ExitStack() as ctx:
        s = sems(nc, ctx, "l2h", X_SEMS + "gathered scaled")
        block = ctx.enter_context(nc.Block())

        @block.gpsimd
        def _(pool):
            for t in range(k.NT):
                pool.indirect_dma_start(out=w.rows[:, t, :], out_offset=None, in_=w.answers,
                                        in_offset=bass.IndirectOffsetOnAxis(ap=w.back[:, t:t + 1], axis=0)).then_inc(s.gathered, 16)
            pipeline(pool, k.NG, [(0, lambda g, m: x_copy_pool(pool, k, s, g, m))])

        @block.vector
        def _(dve):
            dve.wait_ge(s.gathered, 16 * k.NT)

            def new_x(g, m):
                wait(dve, s.x_done, g - 1)
                for j in range(TG):
                    t = TG * g + j
                    last = dve.scalar_tensor_tensor(out=k.xn[:, m, j, :], in0=w.rows[:, bass.ds(t, 1), :], scalar=w.gate[:, bass.ds(t, 1)],
                                                    in1=k.x[:, bass.ds(t, 1), :], op0=ALU.mult, op1=ALU.add)
                last.then_inc(s.xn_ready, 1)
                dve.wait_ge(s.xn_ready, g + 1)
                stats_of_xn(dve, k, s, g, m, TG)

            pipeline(dve, k.NG, [(0, new_x)])


def constant_parts():
    p = np.arange(P)
    n = np.arange(P)
    return {
        "ident": np.eye(P),
        "ones": np.ones((P, P)),
        "frequency": np.broadcast_to((np.float32(1.0) / np.float32(10000.0) ** (np.arange(0, HD, 2, dtype=np.float32) / np.float32(HD))).astype(np.float32), (P, HALF)),
        "count64": np.broadcast_to(np.arange(64.0), (P, 64)),
        "count8": np.broadcast_to(np.arange(8.0) - 8, (P, 8)),
        "before": p[:, None] < n[None, :],
        "token": p[:, None] + P * np.arange(TILES_MAX)[None, :],
        "count16": np.broadcast_to(np.arange(16.0) - 16, (P, 16)),
        "count128": np.broadcast_to(np.arange(128.0) - 128, (P, 128)),
        "same2": np.where(n[None, :] // S == p[:, None] // S, 0.0, NEG),
        "causal2": np.where((n[None, :] % P // S == p[:, None] // S) & (n[None, :] % S <= p[:, None] % S), 0.0, NEG),
        "headmask": (p[:, None] % 32) // HD == np.arange(4)[None, :],
        "causal": np.where(np.arange(4 * S)[None, :] % S > p[:, None] % S, NEG, 0.0),
        "headblock": p[:, None] // HD == n[None, :] // HD,
    }


def constants():
    return np.concatenate([np.asarray(a, np.float32) for a in constant_parts().values()], axis=1)


def constant_columns():
    at, columns = 0, {}
    for name, a in constant_parts().items():
        columns[name] = (at, at + a.shape[1])
        at += a.shape[1]
    return columns


def build_program(nc, dram, tokens):
    NT = tokens // P
    with ExitStack() as ctx:
        k = Core()
        k.dram, k.NT, k.NG = dram, NT, NT // TG
        k.x = ctx.enter_context(nc.sbuf_tensor("x", [P, NT, D], F32))
        k.mv = ctx.enter_context(nc.sbuf_tensor("mean_var", [P, NT, 2], F32))
        k.rstd = ctx.enter_context(nc.sbuf_tensor("rstd", [P, NT], F32))
        k.xn = ctx.enter_context(nc.sbuf_tensor("xn", [P, LANES, TG, D], F32))
        k.xb = ctx.enter_context(nc.sbuf_tensor("xb", [P, LANES, TG, D], F32))
        k.mvn = ctx.enter_context(nc.sbuf_tensor("mvn", [P, LANES, TG, 2], F32))
        k.settled = ctx.enter_context(nc.semaphore("settled"))
        k.started = ctx.enter_context(nc.semaphore("started"))
        k.pad2 = ctx.enter_context(nc.sbuf_tensor("pad2", [P, 1], F32))
        k.pad = ctx.enter_context(nc.sbuf_tensor("pad", [P, 1], F32))
        k.bn6 = ctx.enter_context(nc.sbuf_tensor("bn6", [P, LANES, TG, 6], F32))
        k.consts = ctx.enter_context(nc.sbuf_tensor("consts", [P, dram["consts"].shape[1]], F32))
        k.identb = ctx.enter_context(nc.sbuf_tensor("identb", [P, P], BF16))
        k.same2b = ctx.enter_context(nc.sbuf_tensor("same2b", [P, GT], BF16))
        k.causal2b = ctx.enter_context(nc.sbuf_tensor("causal2b", [P, GT], BF16))
        k.causalb = ctx.enter_context(nc.sbuf_tensor("causalb", [P, 4 * S], BF16))
        columns = constant_columns()

        def constant(name):
            lo, hi = columns[name]
            return k.consts[:, lo:hi]

        k.ident = constant("ident")
        k.ones = constant("ones")
        k.frequency = constant("frequency")
        k.count64 = constant("count64")
        k.count8 = constant("count8")
        k.before = constant("before")
        k.token = constant("token")
        k.count16 = constant("count16")
        k.count128 = constant("count128")
        k.same2 = constant("same2")
        k.causal2 = constant("causal2")
        k.headmask = constant("headmask")
        k.causal = constant("causal")
        k.headblock = constant("headblock")
        k.banks = ctx.enter_context(nc.psum_tensor("banks", [P, 8, BANK], F32))
        k.psum = [k.banks[:, b, :] for b in range(8)]
        phase_start(nc, k)
        phase_l0_attention(nc, k)
        phase_l0_ffn(nc, k)
        phase_l1_attention(nc, k)
        phase_l1_ffn(nc, k)
        phase_l2_attention(nc, k)
        phase_l2_ffn(nc, k)
        phase_l3_attention(nc, k)
        phase_l3_ffn(nc, k)


def kernel(**inputs):
    import numpy as _np
    import concourse.bacc as _bacc
    from concourse import mybir as _mybir
    from concourse.bass_utils import run_bass_kernel_spmd as _run

    nc = _bacc.Bacc("TRN2", target_bir_lowering=False, num_devices=1)
    a = {n: _np.asarray(v) for n, v in inputs.items()}
    tokens = a["x"].shape[0] * a["x"].shape[1]
    lay = {"x": a["x"].reshape(tokens, D), "ctxT": a["ctx_1024"].reshape(tokens, D).T, "consts": constants()}
    for n in ("L0_xattn_Wq", "L0_xattn_Wk", "L0_xattn_Wv", "L0_xattn_Wo"):
        lay[n] = a[n]
    def rows(v):
        return _np.broadcast_to(v[None, :], (P, v.shape[0]))

    for n in "qkvo":
        lay[f"L1_ffn_{n}_proj"] = a[f"L1_ffn_{n}_proj"].transpose(1, 0, 2)
    def swapped(w):
        return w.reshape(D, H, 2, HALF)[:, :, ::-1, :].reshape(D, D)

    w = a["L3_xattn_Wq"]
    lay["L3_xattn_Wq2"] = _np.concatenate([w, swapped(w)], axis=1)
    w = a["L3_xattn_Wkv"]
    lay["L3_xattn_Wk2"] = _np.concatenate([w[:, :D], swapped(w[:, :D])], axis=1)
    lay["L3_xattn_Wv"] = w[:, D:]
    lay["L3_xattn_Wo"] = a["L3_xattn_Wo"]
    pos = a["itok_BxS_0_4095"].reshape(tokens // P, P).T
    lay["positions"] = _np.concatenate([pos, _np.tile(a["L3_xattn_kv_pos_ids"], 2)[:, None]], axis=1)
    lay["segments"] = a["itok_BxS_0_511"].reshape(tokens // P, P).T
    lay["L3_ffn_W_inT"] = a["L3_ffn_W_in"].T.reshape(F0 // P, P, D).transpose(1, 0, 2).reshape(P, F0)
    lay["L3_ffn_W_out"] = a["L3_ffn_W_out"].reshape(F0 // P, P, D).transpose(1, 0, 2).reshape(P, F0)
    lay["L3_ffn_b_in"] = a["L3_ffn_b_in"].reshape(F0 // P, P).T
    lay["L3_ffn_b_out"] = rows(a["L3_ffn_b_out"])
    lay["L2_ffn_wg_coef"] = _np.concatenate([a["L2_ffn_wg"], a["L2_ffn_res_coef"]], axis=1)
    lay["L2_ffn_res_inter_w"] = a["L2_ffn_res_inter_w"]
    lay["L2_ffn_res_inter_b"] = a["L2_ffn_res_inter_b"].reshape(F0 // P, P).T
    lay["L2_ffn_res_output_w"] = a["L2_ffn_res_output_w"].reshape(F0 // P, P, D).transpose(1, 0, 2).reshape(P, F0)
    lay["L2_ffn_res_output_b"] = rows(a["L2_ffn_res_output_b"])
    lay["L2_ffn_attn_nw"] = a["L2_ffn_attn_nw"][:, None]
    lay["L2_ffn_attn_nb"] = a["L2_ffn_attn_nb"][:, None]
    lay["L2_ffn_expert_sets"] = _np.concatenate([
        a["L2_ffn_inter_w"].reshape(8, P, F0),
        a["L2_ffn_output_w"].reshape(8, F0 // P, P, D).transpose(0, 2, 1, 3).reshape(8, P, F0),
        a["L2_ffn_inter_b"].reshape(8, F0 // P, P).transpose(0, 2, 1),
        _np.broadcast_to(a["L2_ffn_output_b"][:, None, :], (8, P, D))], axis=2).reshape(8 * P, -1)
    lay["L2_xattn_WqT"] = a["L2_xattn_Wq"].T
    lay["L2_xattn_WcT"] = a["L2_xattn_Wc"].T
    kv = a["L2_xattn_Wkv"].T
    lay["L2_xattn_WkvT_heads"] = _np.concatenate([_np.tile(kv[:, :HD], H), _np.tile(kv[:, HD:], H)], axis=1)
    lay["L1_ffn_sim_matrix"] = a["L1_ffn_sim_matrix"]
    lay["L1_ffn_gates"] = rows(a["L1_ffn_gates"])
    q = _np.arange(P)[:, None, None]
    lay["selector"] = ((q % 32 == _np.arange(16)[None, :, None]) & (q < 96) & _np.ones((1, 1, P), bool)).astype(_np.float32).reshape(P, 16 * P)
    lay["zero_row"] = _np.zeros((P, D), _np.float32)
    lay["zero_column"] = _np.zeros((P, 1), _np.float32)
    for n in "qkvo":
        lay[f"L1_xattn_W{n}T"] = a[f"L1_xattn_W{n}"].T
    for n in "qk":
        lay[f"L1_xattn_b{n}"] = a[f"L1_xattn_b{n}"][:, None]
    lay["L1_xattn_bv"] = a["L1_xattn_bv"][:, None]
    lay["L1_xattn_bo"] = rows(a["L1_xattn_bo"])
    lay["L0_ffn_w1T"] = a["L0_ffn_w1"].T
    lay["L0_ffn_w2T"] = a["L0_ffn_w2"].T.reshape(F0 // P, P, D).transpose(1, 0, 2).reshape(P, F0)
    lay["L0_ffn_b1"] = rows(a["L0_ffn_b1"])
    lay["L0_ffn_b2"] = rows(a["L0_ffn_b2"])
    for n in ("L0_xattn_bq", "L0_xattn_bk", "L0_xattn_bo"):
        lay[n + "_x4"] = _np.tile(a[n], TG)[None, :]
    lay["L0_xattn_bv"] = a["L0_xattn_bv"][:, None]
    arrays, aps = {}, {}
    for n, v in lay.items():
        v = _np.ascontiguousarray(v)
        arrays[f"in_{n}"] = v
        aps[n] = nc.dram_tensor(f"in_{n}", v.shape, _mybir.dt.from_np(v.dtype), kind="ExternalInput").ap()
    aps["out"] = nc.dram_tensor("out_0", (tokens, D), F32, kind="ExternalOutput").ap()
    build_program(nc, aps, tokens)
    r = _run(nc, [arrays], core_ids=[0])
    return r.results[0]["out_0"].reshape(a["x"].shape)
```
